# Optimizing a Trainium2 kernel written in Bass

```python
import numpy as np
import jax
import jax.numpy as jnp

def _softmax(x, axis=-1):
    return jax.nn.softmax(x, axis=axis)

def _gelu(x):
    return jax.nn.gelu(x, approximate=True)

def _silu(x):
    return jax.nn.silu(x)

def _sigmoid(x):
    return jax.nn.sigmoid(x)

def _layernorm(x, axis=-1, eps=1e-05):
    m = jnp.mean(x, axis=axis, keepdims=True)
    v = jnp.var(x, axis=axis, keepdims=True)
    return (x - m) / jnp.sqrt(v + eps)

def _scatter_add(tgt, idx, src, axis=0):
    return tgt.at[idx].add(src)

def _segment_sum(src, seg, n):
    return jax.ops.segment_sum(src, seg, n)
kernel_name = 'mk_gnn_resnorm_d1_gnn_r8_602edb'

def setup_inputs(seed: int=0):
    np.random.seed(seed)
    _w = jnp.asarray

    def _rec_inputs():
        import jax
        import jax.numpy as jnp
        _gk = jax.random.key(seed)
        x = -0.0003713 + 1 * jax.random.normal(jax.random.fold_in(_gk, 1), (6250, 128), jnp.float32)
        _s = jax.random.randint(jax.random.fold_in(_gk, 2), (50000,), 0, 6250, jnp.int32)
        _d = jax.random.randint(jax.random.fold_in(_gk, 3), (50000,), 0, 6250, jnp.int32)
        _loop = jnp.arange(6250, dtype=jnp.int32)
        src = jnp.concatenate([_s, _d, _loop])
        dst = jnp.concatenate([_d, _s, _loop])
        _o = jnp.argsort(dst, stable=True)
        src = src[_o]
        dst = dst[_o]
        edge_attr_64 = 0.000102155 + 1.00015 * jax.random.normal(jax.random.fold_in(_gk, 11), (106250, 64), jnp.float32)
        edge_weight = jax.random.uniform(jax.random.fold_in(_gk, 13), (106250,), jnp.float32, 0.0, 0.999999)
        return (x, src, dst, edge_attr_64, edge_weight)
    x, src, dst, edge_attr_64, edge_weight = _rec_inputs()

    def _L0_gnn_setup():
        import jax, jax.numpy as jnp
        import numpy as np
        N_NODES = 12500
        N_EDGES = 62500
        IN_CH = 128
        EDGE_CH = 64

        def _glorot(key, shape):
            fan_in, fan_out = (shape[0], shape[1])
            lim = (6.0 / (fan_in + fan_out)) ** 0.5
            return jax.random.uniform(key, shape, jnp.float32, -lim, lim)
        key = jax.random.key(seed)
        ks = jax.random.split(key, 14)
        x = jax.random.normal(ks[0], (N_NODES, IN_CH), jnp.float32)
        edge_index = jax.random.randint(ks[1], (2, N_EDGES), 0, N_NODES, jnp.int64)
        edge_attr = jax.random.normal(ks[2], (N_EDGES, EDGE_CH), jnp.float32)
        timestamps = jax.random.uniform(ks[3], (N_EDGES,), jnp.float32)
        We1 = _glorot(ks[4], (EDGE_CH, 2 * EDGE_CH))
        be1 = jnp.zeros((2 * EDGE_CH,), jnp.float32)
        We2 = _glorot(ks[5], (2 * EDGE_CH, IN_CH))
        be2 = jnp.zeros((IN_CH,), jnp.float32)
        Wt = _glorot(ks[6], (1, IN_CH))
        bt = jnp.zeros((IN_CH,), jnp.float32)
        Wn1 = _glorot(ks[7], (2 * IN_CH, IN_CH))
        bn1 = jnp.zeros((IN_CH,), jnp.float32)
        Wn2 = _glorot(ks[8], (IN_CH, IN_CH))
        bn2 = jnp.zeros((IN_CH,), jnp.float32)
        return {'x': x, 'edge_index': edge_index, 'edge_attr': edge_attr, 'timestamps': timestamps, 'We1': We1, 'be1': be1, 'We2': We2, 'be2': be2, 'Wt': Wt, 'bt': bt, 'Wn1': Wn1, 'bn1': bn1, 'Wn2': Wn2, 'bn2': bn2}
    _L0_gnn_all = _L0_gnn_setup()
    _L0_gnn_in = {k: v for k, v in _L0_gnn_all.items() if k in ('We1', 'be1', 'We2', 'be2', 'Wt', 'bt', 'Wn1', 'bn1', 'Wn2', 'bn2')}
    del _L0_gnn_all
    return {'x': x, 'src': src, 'dst': dst, 'edge_attr_64': edge_attr_64, 'edge_weight': edge_weight, 'L0_gnn_We1': _L0_gnn_in['We1'], 'L0_gnn_be1': _L0_gnn_in['be1'], 'L0_gnn_We2': _L0_gnn_in['We2'], 'L0_gnn_be2': _L0_gnn_in['be2'], 'L0_gnn_Wt': _L0_gnn_in['Wt'], 'L0_gnn_bt': _L0_gnn_in['bt'], 'L0_gnn_Wn1': _L0_gnn_in['Wn1'], 'L0_gnn_bn1': _L0_gnn_in['bn1'], 'L0_gnn_Wn2': _L0_gnn_in['Wn2'], 'L0_gnn_bn2': _L0_gnn_in['bn2']}

def reference(x, src, dst, edge_attr_64, edge_weight, L0_gnn_We1, L0_gnn_be1, L0_gnn_We2, L0_gnn_be2, L0_gnn_Wt, L0_gnn_bt, L0_gnn_Wn1, L0_gnn_bn1, L0_gnn_Wn2, L0_gnn_bn2):
    import jax
    import jax.numpy as jnp

    def _L0_gnn_ref(x, edge_index, edge_attr, timestamps, We1, be1, We2, be2, Wt, bt, Wn1, bn1, Wn2, bn2):
        import jax, jax.numpy as jnp
        import numpy as np
        N_NODES = 12500
        N_EDGES = 62500
        IN_CH = 128
        EDGE_CH = 64

        def _glorot(key, shape):
            fan_in, fan_out = (shape[0], shape[1])
            lim = (6.0 / (fan_in + fan_out)) ** 0.5
            return jax.random.uniform(key, shape, jnp.float32, -lim, lim)
        ts = timestamps[:, None]
        ef = jax.nn.relu(edge_attr @ We1 + be1) @ We2 + be2
        tw = jax.nn.sigmoid(ts @ Wt + bt)
        ef = ef * tw
        row, col = (edge_index[0], edge_index[1])
        combined = jnp.concatenate([x[row], ef], axis=1)
        msg = jax.nn.relu(combined @ Wn1 + bn1) @ Wn2 + bn2
        out = jax.ops.segment_sum(msg, col, num_segments=x.shape[0])
        return out + x
    edge_index = jnp.stack([src, dst])
    x = _layernorm(x + _L0_gnn_ref(x, edge_index, edge_attr_64, edge_weight, L0_gnn_We1, L0_gnn_be1, L0_gnn_We2, L0_gnn_be2, L0_gnn_Wt, L0_gnn_bt, L0_gnn_Wn1, L0_gnn_bn1, L0_gnn_Wn2, L0_gnn_bn2), axis=-1)
    return x

_drawn_inputs = setup_inputs


def setup_inputs(seed=0):
    import zlib

    import numpy as np

    out = dict(_drawn_inputs(seed))
    spreads = {'L0_gnn_be1': (0.0, 0.1),
     'L0_gnn_be2': (0.0, 0.1),
     'L0_gnn_bt': (0.0, 0.678),
     'L0_gnn_bn1': (0.0, 0.1),
     'L0_gnn_bn2': (0.0, 0.1)}
    factors = {'edge_weight': 8.0, 'L0_gnn_Wt': 7.903}
    for name, (base, spread) in spreads.items():
        noise = np.random.default_rng([zlib.crc32(name.encode()), seed]).standard_normal(out[name].shape)
        drawn = base * np.exp(spread * noise) if base else spread * noise
        out[name] = jnp.asarray(drawn.astype(out[name].dtype))
    for name, factor in factors.items():
        out[name] = (out[name] * factor).astype(out[name].dtype)
    return out
```

```python
from contextlib import ExitStack

import concourse.bass as bass
from concourse import mybir

ALU = mybir.AluOpType
ACT = mybir.ActivationFunctionType
AX_X = mybir.AxisListType.X
F32 = mybir.dt.float32
BF16 = mybir.dt.bfloat16
I32 = mybir.dt.int32
DVE_ENGINE = mybir.EngineType.DVE
PE_ENGINE = mybir.EngineType.PE

P = 128
TILES = 4
GE = TILES * P
N_WEIGHTS = 11
SG = 4
SE = SG * GE
W = 64
EPS = 1e-5
NT = 125
BT = 4
XCH = 10
PARTS = 3
ORDER = [0, 2, 1, 3]


def gnn_kernel(nc, x, src, dst, edge_attr, edge_weight, We1, be1, We2, be2, Wt, bt, Wn1, bn1, Wn2, bn2, out):
    N, C = x.shape
    E, F = edge_attr.shape
    SUPERS = 1 + E // SE
    G = SUPERS * SG
    SHARED = SUPERS * SE - E
    BODY = 2 * SG
    TURNS = SUPERS // 2
    ROWS = [P, G - P]
    NTILES = N // NT
    BLOCKS = [(t, min(BT, NTILES - t)) for t in range(0, NTILES, BT)]
    CHUNKS = NTILES // XCH
    assert C == P and F == 64 and E % SE and SUPERS % 2 == 0 and P < G <= 2 * P
    assert N % NT == 0 and NTILES % XCH == 0 and 0 < SHARED <= GE

    table = nc.dram_tensor("node_table", (N, C), F32).ap()
    t_parts = nc.dram_tensor("t_parts", (PARTS, G, GE), BF16).ap()
    spans_dram = nc.dram_tensor("spans_dram", (G, 2), I32).ap()

    with ExitStack() as ctx:
        def sb(name, shape, dt=F32):
            return ctx.enter_context(nc.sbuf_tensor(name, shape, dt))

        def psum(name, shape):
            return ctx.enter_context(nc.psum_tensor(name, shape, F32))

        def sem(name):
            return ctx.enter_context(nc.semaphore(name))

        ident = sb("ident", [P, P])
        ones_parts = sb("ones_parts", [PARTS, P], BF16)
        node_ids = sb("node_ids", [P, N + W])
        we1 = sb("we1", [P, C])
        we2 = sb("we2", [P, C])
        wn1 = sb("wn1", [P, 2, C])
        wn2 = sb("wn2", [P, C])
        be1_c, be2_c, wt_c, bt_c = (sb(n, [P, 1]) for n in ("be1_c", "be2_c", "wt_c", "bt_c"))
        bn1_all = sb("bn1_all", [P, C])
        bn2_all = sb("bn2_all", [P, C])
        x_sb = sb("x_sb", [NT, NTILES, C])
        table_sb = sb("table_sb", [NT, 3, BT, C])
        sums = sb("sums", [P, N + W])
        counts = sb("counts", [P, N + W])
        stats = sb("stats", [NT, NTILES, 6])
        mean_var = sb("mean_var", [NT, NTILES, 2])
        std, rstd, shift = (sb(n, [NT, NTILES]) for n in ("std", "rstd", "shift"))
        eps_c = sb("eps_c", [P, 1])
        src_rows = sb("src_rows", [P, 2, GE], I32)
        dst_rows = sb("dst_rows", [P, 2, GE], I32)
        t_split = sb("t_split", [P, 2, PARTS, GE], BF16)
        span_f = sb("span_f", [P, 2, 2])
        span_i = sb("span_i", [P, 2, 2], I32)
        src_e = sb("src_e", [P, G + BODY, TILES])
        dst_e = sb("dst_e", [P, G, TILES])
        spans = sb("spans", [1, G, 2], I32)
        widths = sb("widths", [1, G])
        widest = sb("widest", [1, SUPERS], I32)
        ea = [sb(f"ea{i}", [P, SG, TILES * F]) for i in range(2)]
        tp = [sb(f"tp{i}", [PARTS, SG, GE], BF16) for i in range(2)]
        idx = [sb(f"idx{i}", [P, SG * TILES], I32) for i in range(2)]
        eaT = sb("eaT", [P, 2, 2, P])
        h1 = sb("h1", [P, 2, 2, GE // 2])
        tw = sb("tw", [P, 2, GE])
        efw = sb("efw", [P, 2, GE])
        gathered = sb("gathered", [P, BODY, GE])
        pre = sb("pre", [P, 2, GE])
        h = sb("h", [P, BODY, GE])
        onehot = sb("onehot", [P, 2, TILES, W])
        onehot_more = sb("onehot_more", [P, TILES, W])
        hits = sb("hits", [P, 2, W])
        hits_more = sb("hits_more", [P, W])
        ids_f = h[:, 0:4, :].rearrange("p (a b) e -> p a b e", a=2)
        t_left = h[:, 4:6, :]
        t_rows = h[:, 6:8, :]
        xT = efw[:, :, :].rearrange("p b (t n) -> p b t n", t=BT)

        psT = psum("psT", [P, 2, P])
        psH = psum("psH", [P, 2, 512])
        psB = psum("psB", [P, GE])
        psE = psum("psE", [P, GE])
        psM = psum("psM", [P, GE])
        psA = psum("psA", [P, 512])
        psX = psum("psX", [P, 512])
        banks = [psE, psM]

        weights_in, src_in, dst_in, t_in = (sem(n) for n in ("weights_in", "src_in", "dst_in", "t_in"))
        x_in = [sem(f"x_in{i}") for i in range(CHUNKS)]
        table_out = [sem(f"table_out{i}") for i in range(3)]
        t_out, span_out, spans_in = sem("t_out"), sem("span_out"), sem("spans_in")
        edges_in = [sem(f"edges_in{i}") for i in range(2)]
        gather_in = [sem(f"gather_in{i}") for i in range(BODY)]
        y_out = sem("y_out")
        ident_ready, ones_ready, node_ids_ready, tables_zero = (
            sem(n) for n in ("ident_ready", "ones_ready", "node_ids_ready", "tables_zero"))
        xT_ps, xT_ready, table_ps, table_ready = (sem(n) for n in ("xT_ps", "xT_ready", "table_ps", "table_ready"))
        src_cast, dst_cast, dst_masked = sem("src_cast"), sem("dst_cast"), sem("dst_masked")
        ids_ps, src_e_ready, dst_e_ready = sem("ids_ps"), sem("src_e_ready"), sem("dst_e_ready")
        split_step, span_found, span_ready, spans_ready = (
            sem(n) for n in ("split_step", "span_found", "span_ready", "spans_ready"))
        idx_ready = sem("idx_ready")
        eaT_ps, eaT_ready, h1_ps, h1_ready = (sem(n) for n in ("eaT_ps", "eaT_ready", "h1_ps", "h1_ready"))
        t_ps, tw_ready, ef_ps, efw_ready = (sem(n) for n in ("t_ps", "tw_ready", "ef_ps", "efw_ready"))
        msg_ps, pre_ready, h_ready = (sem(n) for n in ("msg_ps", "pre_ready", "h_ready"))
        onehot_ready, hits_ready, counts_added = (sem(n) for n in ("onehot_ready", "hits_ready", "counts_added"))
        sum_ps, sums_added = sem("sum_ps"), sem("sums_added")
        more_onehot, more_hits, more_counted, more_sum, more_added = (
            sem(n) for n in ("more_onehot", "more_hits", "more_counted", "more_sum", "more_added"))
        y_ps, y_ready, stats_ready, moments_ready = (sem(n) for n in ("y_ps", "y_ready", "stats_ready", "moments_ready"))
        std_ready, rstd_ready, shift_ready, y_done = (sem(n) for n in ("std_ready", "rstd_ready", "shift_ready", "y_done"))

        block = ctx.enter_context(nc.Block())

        x_tiles = x.rearrange("(t n) c -> n t c", n=NT)
        out_tiles = out.rearrange("(t n) c -> n t c", n=NT)
        table_tiles = table.rearrange("(t n) c -> n t c", n=NT)

        def wait(eng, semaphore, value):
            if not (isinstance(value, int) and value <= 0):
                eng.wait_ge(semaphore, value)

        def live(i, k, lag):
            return not isinstance(i, int) or (k >= lag if i == 0 else k < lag)

        def main_loop(eng, step, depth):
            for k in range(BODY):
                step(0, k)
            with eng.Fori(1, TURNS) as i:
                for k in range(BODY):
                    step(i, k)
            for k in range(depth):
                step(TURNS, k)

        def span_of(engine, g):
            return (nc.values_load(spans[0:1, bass.ds(g, 1), 0], engines=(engine,), min_val=0, max_val=N - 1),
                    nc.values_load(spans[0:1, bass.ds(g, 1), 1], engines=(engine,), min_val=0, max_val=N - 1))

        def least_of(engine, g):
            return nc.values_load(spans[0:1, bass.ds(g, 1), 0], engines=(engine,), min_val=0, max_val=N - 1)

        def by_group(a):
            return [a[E - SE:E].rearrange("(g e) -> g e", e=GE),
                    a[0:(P - SG) * GE].rearrange("(g e) -> g e", e=GE),
                    a[(P - SG) * GE:(G - SG) * GE].rearrange("(g e) -> g e", e=GE)]

        @block.sync
        def _(sp):
            def load_rows(tile, a, landed):
                last, first, second = by_group(a)
                sp.dma_start(tile[0:SG, 0, :], last).then_inc(landed, 16)
                sp.dma_start(tile[SG:P, 0, :], first).then_inc(landed, 16)
                sp.dma_start(tile[0:ROWS[1], 1, :], second).then_inc(landed, 16)

            load_rows(src_rows, src, src_in)
            for c in range(CHUNKS):
                sp.dma_start(x_sb[:, c * XCH:(c + 1) * XCH, :],
                             x_tiles[:, c * XCH:(c + 1) * XCH, :]).then_inc(x_in[c], 16)
                if c == 0:
                    load_rows(dst_rows, dst, dst_in)
                if c == 1:
                    load_rows(t_rows, edge_weight, t_in)
            sp.wait_ge(span_ready, 2)
            for b in range(2):
                sp.dma_start(spans_dram[b * P:b * P + ROWS[b], :], span_i[0:ROWS[b], b, :]).then_inc(span_out, 16)
            sp.wait_ge(span_out, 32)
            sp.dma_start(spans[:, :, :], spans_dram.rearrange("(a g) k -> a g k", a=1)).then_inc(spans_in, 16)
            sp.wait_ge(split_step, 12)
            for b in range(2):
                sp.dma_start(t_parts[:, b * P:b * P + ROWS[b], :].rearrange("k g e -> g k e"),
                             t_split[0:ROWS[b], b, :, :]).then_inc(t_out, 16)

            def load_super(m, slot, start):
                if not isinstance(m, int):
                    sp.wait_ge(eaT_ps, (m - 1) * SG)
                    sp.wait_ge(t_ps, (m - 1) * SG)
                sp.dma_start(ea[slot][:, :, :],
                             edge_attr[bass.ds(start, SE), :].rearrange("(g p j) f -> p g (j f)", p=P, j=TILES))\
                    .then_inc(edges_in[slot], 16)
                if isinstance(m, int) and m == 0:
                    sp.wait_ge(t_out, 32)
                sp.dma_start(tp[slot][:, :, :], t_parts[:, bass.ds(m * SG, SG), :]).then_inc(edges_in[slot], 16)

            load_super(0, 0, E - SE)
            load_super(1, 1, 0)
            with sp.Fori(1, TURNS) as i:
                load_super(i * 2, 0, i * (2 * SE) - SE)
                load_super(i * 2 + 1, 1, i * (2 * SE))

            for c in range(CHUNKS):
                sp.wait_ge(y_done, (c + 1) * XCH)
                sp.dma_start(out_tiles[:, c * XCH:(c + 1) * XCH, :],
                             x_sb[:, c * XCH:(c + 1) * XCH, :]).then_inc(y_out, 16)
            sp.wait_ge(y_out, 16 * CHUNKS)

        @block.gpsimd
        def _(pool):
            pool.memset(ident[:, :], 0.0).then_inc(ident_ready, 1)
            pool.wait_ge(ident_ready, 1)
            pool.affine_select(out=ident[:, :], in_=ident[:, :], compare_op=ALU.not_equal, fill=1.0,
                               base=0, pattern=[[-1, P]], channel_multiplier=1).then_inc(ident_ready, 1)
            pool.memset(ones_parts[:, :], 1.0).then_inc(ones_ready, 1)
            pool.memset(eps_c[:, :], EPS).then_inc(ones_ready, 1)
            pool.iota(node_ids[:, :], pattern=[[1, N + W]], base=0, channel_multiplier=0,
                      allow_small_or_imprecise_dtypes=True).then_inc(node_ids_ready, 1)
            pool.memset(sums[:, :], 0.0).then_inc(tables_zero, 1)
            pool.memset(counts[:, :], 0.0).then_inc(tables_zero, 1)
            for r in range(3):
                pool.wait_ge(table_out[r], 16 * len(BLOCKS[r::3]))

            def gather_super(m, slot):
                pool.wait_ge(idx_ready, m + 1)
                pool.nop(nofuse=True)
                for q in range(SG):
                    place = slot * SG + q
                    if not isinstance(m, int):
                        pool.wait_ge(pre_ready, (m - 2) * SG + (q + 1))
                        pool.nop(nofuse=True)
                    for t in range(TILES):
                        n = q * TILES + t
                        pool.indirect_dma_start(
                            gathered[:, place, t * C:(t + 1) * C], None, table,
                            bass.IndirectOffsetOnAxis(idx[slot][:, n:n + 1], 0)).then_inc(gather_in[place], 16)

            gather_super(0, 0)
            gather_super(1, 1)
            with pool.Fori(1, TURNS) as i:
                gather_super(i * 2, 0)
                gather_super(i * 2 + 1, 1)

        @block.scalar
        def _(act):
            col, row = "(c a) -> c a", "(a c) -> a c"
            loads = [(wn1[:, :, :], Wn1.rearrange("(a k) c -> k a c", k=P)),
                     (bn1_all[:, :], bn1.rearrange(row, a=1).to_broadcast([P, C])),
                     (we1[0:F, :], We1), (we1[F:2 * F, :], We1), (we2[:, :], We2),
                     (be1_c[:, :], be1.rearrange(col, a=1)), (be2_c[:, :], be2.rearrange(col, a=1)),
                     (bt_c[:, :], bt.rearrange(col, a=1)), (wt_c[:, :], Wt.rearrange("a c -> c a")),
                     (wn2[:, :], Wn2), (bn2_all[:, :], bn2.rearrange(row, a=1).to_broadcast([P, C]))]
            assert len(loads) == N_WEIGHTS
            for to, of in loads:
                act.dma_start(to, of).then_inc(weights_in, 16)

            def store_table(b):
                t0, n = BLOCKS[b]
                act.wait_ge(table_ready, b + 1)
                act.dma_start(table_tiles[:, t0:t0 + n, :], table_sb[:, b % 3, 0:n, :])\
                    .then_inc(table_out[b % 3], 16)

            for b, (t0, n) in enumerate(BLOCKS):
                act.wait_ge(xT_ps, b + 1)
                if b >= 2:
                    act.wait_ge(table_ps, b - 1)
                nc.scalar.activation(xT[:, b % 2, 0:n, 0:NT],
                                     psH[:, b % 2, :].rearrange("p (t n) -> p t n", t=BT)[:, 0:n, 0:NT],
                                     ACT.Copy).then_inc(xT_ready, 1)
                if b >= 1:
                    store_table(b - 1)
            store_table(len(BLOCKS) - 1)
            act.wait_ge(weights_in, 16 * N_WEIGHTS)

            def step(i, k):
                if live(i, k, 0) and not (isinstance(i, int) and i == TURNS):
                    g = i * BODY + k
                    act.wait_ge(eaT_ps, g + 1)
                    wait(act, h1_ps, g - 1)
                    nc.scalar.activation(eaT[:, k % 2, :, :], psT[:, :, :], ACT.Copy).then_inc(eaT_ready, 1)
                if live(i, k, 1):
                    g = i * BODY + (k - 1)
                    act.wait_ge(h1_ps, g + 1)
                    wait(act, ef_ps, g - 1)
                    nc.scalar.activation(h1[:, (k - 1) % 2, :, :], psH[:, :, 0:GE // 2], ACT.Relu,
                                         bias=be1_c[:, :]).then_inc(h1_ready, 1)
                    act.wait_ge(t_ps, g + 1)
                    wait(act, efw_ready, g - 1)
                    nc.scalar.activation(tw[:, (k - 1) % 2, :], psB[:, :], ACT.Sigmoid, bias=bt_c[:, :],
                                         scale=wt_c[:, :]).then_inc(tw_ready, 1)
                if live(i, k, 3):
                    g = i * BODY + (k - 3)
                    act.wait_ge(pre_ready, g + 1)
                    if (k - 3) % SG == 0:
                        wait(act, sum_ps, g - SG)
                    nc.scalar.activation(h[:, (k - 3) % BODY, :], pre[:, (k - 3) % 2, :], ACT.Relu).then_inc(h_ready, 1)

            act.wait_ge(split_step, 12)
            act.wait_ge(ids_ps, 4)
            main_loop(act, step, 3)

            def normalize(b):
                t0, n = BLOCKS[b]
                act.wait_ge(shift_ready, b + 1)
                for t in range(t0, t0 + n):
                    nc.scalar.activation(x_sb[:, t, :], x_sb[:, t, :], ACT.Identity, bias=shift[:, t:t + 1],
                                         scale=rstd[:, t:t + 1]).then_inc(y_done, 1)

            act.wait_ge(ones_ready, 2)
            for b, (t0, n) in enumerate(BLOCKS):
                act.wait_ge(moments_ready, (t0 + n))
                nc.scalar.activation(std[:, t0:t0 + n], mean_var[:, t0:t0 + n, 1], ACT.Sqrt,
                                     bias=eps_c[0:NT, :]).then_inc(std_ready, 1)
                if b >= 1:
                    normalize(b - 1)
            normalize(len(BLOCKS) - 1)

        @block.tensor
        def _(pe):
            def transpose_ids(a, b, bank):
                rows = ids_f[0:ROWS[b], a, b, :].rearrange("g (p j) -> g j p", j=TILES)
                for q, j in enumerate(ORDER):
                    mm = nc.tensor.transpose(bank[:, q * P:q * P + ROWS[b]], rows[:, j, :],
                                             ident[0:ROWS[b], 0:ROWS[b]])
                mm.then_inc(ids_ps, 1)

            pe.wait_ge(ident_ready, 2)
            pe.wait_ge(src_cast, 2)
            transpose_ids(0, 0, psX)
            transpose_ids(0, 1, psA)

            def transpose_x(b):
                t0, n = BLOCKS[b]
                for c in range(t0 // XCH, (t0 + n - 1) // XCH + 1):
                    pe.wait_ge(x_in[c], 16)
                if b >= 2:
                    pe.wait_ge(xT_ready, b - 1)
                for q in range(n):
                    mm = nc.tensor.transpose(psH[:, b % 2, q * P:q * P + NT], x_sb[:, t0 + q, :], ident[0:NT, 0:NT])
                mm.then_inc(xT_ps, 1)

            def multiply_x(b):
                t0, n = BLOCKS[b]
                pe.wait_ge(xT_ready, b + 1)
                if b >= 2:
                    pe.wait_ge(table_ready, b - 1)
                for q in range(n):
                    mm = nc.tensor.matmul(banks[b % 2][0:NT, q * P:(q + 1) * P], xT[:, b % 2, q, 0:NT], wn1[:, 0, :],
                                          start=True, stop=True)
                mm.then_inc(table_ps, 1)

            transpose_x(0)
            pe.wait_ge(weights_in, 16 * N_WEIGHTS)
            for b in range(len(BLOCKS)):
                if b + 1 < len(BLOCKS):
                    transpose_x(b + 1)
                multiply_x(b)

            pe.wait_ge(dst_masked, 1)
            for b, bank in enumerate((psX, psA)):
                pe.wait_ge(src_e_ready, b + 1)
                transpose_ids(1, b, bank)

            windows = pe.alloc_register("pe_windows")
            pe.reg_mov(windows, 0)

            def more_windows(m, g, place):
                wide = nc.values_load(widest[0:1, bass.ds(m, 1)], engines=(PE_ENGINE,), min_val=0, max_val=N - 1)
                with pe.If(wide >= W):
                    wait(pe, sums_added, g)
                    for q in range(SG):
                        lo, hi = span_of(PE_ENGINE, m * SG + q)
                        with pe.If(hi - lo >= W):
                            with pe.Fori(lo + W, hi + 1, W):
                                pe.reg_add(windows, windows, 1)
                                n = pe.snap(windows, min_val=1)
                                pe.wait_ge(more_onehot, n)
                                for t in range(TILES):
                                    mm = nc.tensor.matmul(psA[:, 0:W], h[:, place + q, t * C:(t + 1) * C],
                                                          onehot_more[:, t, :], start=(t == 0), stop=(t == TILES - 1))
                                mm.then_inc(more_sum, 1)
                                pe.wait_ge(more_added, n)

            def step(i, k):
                if live(i, k, 0) and not (isinstance(i, int) and i == TURNS):
                    g = i * BODY + k
                    if k % SG == 0:
                        pe.wait_ge(edges_in[k // SG], i * 32 + 32)
                    wait(pe, eaT_ready, g)
                    for a in range(2):
                        mm = nc.tensor.transpose(psT[:, a, :], ea[k // SG][:, k % SG, a * P:(a + 1) * P], ident[:, :])
                    mm.then_inc(eaT_ps, 1)
                if live(i, k, 1):
                    g = i * BODY + (k - 1)
                    pe.wait_ge(eaT_ready, g + 1)
                    wait(pe, h1_ready, g)
                    for a in range(2):
                        mm = nc.tensor.matmul(psH[:, a, 0:GE // 2], we1[a * F:(a + 1) * F, :],
                                              eaT[a * F:(a + 1) * F, (k - 1) % 2, :, :], start=True, stop=True)
                    mm.then_inc(h1_ps, 1)
                    wait(pe, tw_ready, g)
                    nc.tensor.matmul(psB[:, :], ones_parts[:, :], tp[(k - 1) // SG % 2][:, (k - 1) % SG, :],
                                     start=True, stop=True).then_inc(t_ps, 1)
                if live(i, k, 2):
                    g = i * BODY + (k - 2)
                    pe.wait_ge(h1_ready, g + 1)
                    wait(pe, efw_ready, g)
                    nc.tensor.matmul(psE[:, :], we2[:, :], h1[:, (k - 2) % 2, :, :], start=True, stop=True)\
                        .then_inc(ef_ps, 1)
                if live(i, k, 3):
                    g = i * BODY + (k - 3)
                    pe.wait_ge(efw_ready, g + 1)
                    wait(pe, pre_ready, g)
                    for t in range(TILES):
                        mm = nc.tensor.matmul(psM[:, t * P:(t + 1) * P], efw[:, (k - 3) % 2, t * P:(t + 1) * P],
                                              wn1[:, 1, :], start=True, stop=True)
                    mm.then_inc(msg_ps, 1)
                if live(i, k, 4):
                    g = i * BODY + (k - 4)
                    pe.wait_ge(h_ready, g + 1)
                    if k % SG == SG - 1:
                        more_windows(i * 2 + (k - 4) // SG, g, (k - 4) // SG % 2 * SG)
                    pe.wait_ge(onehot_ready, g + 1)
                    wait(pe, sums_added, g)
                    for t in range(TILES):
                        mm = nc.tensor.matmul(psA[:, 0:W], h[:, (k - 4) % BODY, t * C:(t + 1) * C],
                                              onehot[:, (k - 4) % 2, t, :], start=(t == 0), stop=(t == TILES - 1))
                    mm.then_inc(sum_ps, 1)

            pe.wait_ge(dst_e_ready, 2)
            pe.wait_ge(table_ready, len(BLOCKS))
            pe.wait_ge(spans_ready, 2)
            pe.wait_ge(ones_ready, 1)
            main_loop(pe, step, 4)

            pe.wait_ge(sums_added, G)
            pe.wait_ge(counts_added, G)
            for b, (t0, n) in enumerate(BLOCKS):
                if b >= 2:
                    pe.wait_ge(y_ready, b - 1)
                for q in range(n):
                    at = slice((t0 + q) * NT, (t0 + q + 1) * NT)
                    rows = banks[b % 2][0:NT, q * P:(q + 1) * P]
                    nc.tensor.matmul(rows, sums[:, at], wn2[:, :], start=True, stop=False)
                    mm = nc.tensor.matmul(rows, counts[:, at], bn2_all[:, :], start=False, stop=True)
                mm.then_inc(y_ps, 1)

        @block.vector
        def _(dve):
            for a, rows, landed, cast in ((0, src_rows, src_in, src_cast), (1, dst_rows, dst_in, dst_cast)):
                dve.wait_ge(landed, 48)
                for b in range(2):
                    nc.vector.tensor_copy(ids_f[0:ROWS[b], a, b, :], rows[0:ROWS[b], b, :]).then_inc(cast, 1)

            nc.vector.memset(src_e[:, G:G + BODY, :], 0.0)

            def spread(ids, b, bank, ready):
                nc.vector.tensor_copy(ids[:, b * P:b * P + ROWS[b], :].rearrange("p g q -> p q g"),
                                      bank[:, :].rearrange("p (q g) -> p q g", q=TILES)[:, :, 0:ROWS[b]])\
                    .then_inc(ready, 1)

            def stage_indices(m, slot):
                nc.vector.tensor_copy(idx[slot][:, :], src_e[:, bass.ds(m * SG, SG), :].rearrange("p g q -> p (g q)"))\
                    .then_inc(idx_ready, 1)

            for b, bank in enumerate((psX, psA)):
                dve.wait_ge(ids_ps, b + 1)
                spread(src_e, b, bank, src_e_ready)
            dve.wait_ge(src_e_ready, 2)
            stage_indices(0, 0)
            stage_indices(1, 1)

            dve.wait_ge(dst_cast, 2)
            for b in range(2):
                for n, op in enumerate((ALU.min, ALU.max)):
                    nc.vector.tensor_reduce(span_f[0:ROWS[b], b, n:n + 1], ids_f[0:ROWS[b], 1, b, :], AX_X, op)\
                        .then_inc(span_found, 1)
            dve.wait_ge(span_found, 4)
            for b in range(2):
                nc.vector.tensor_copy(span_i[0:ROWS[b], b, :], span_f[0:ROWS[b], b, :]).then_inc(span_ready, 1)
            nc.vector.memset(ids_f[0:1, 1, 0, 0:SHARED], -1.0).then_inc(dst_masked, 1)

            dve.wait_ge(t_in, 48)

            def split_t(s):
                b, part = s % 2, s // 2
                R = ROWS[b]
                left = t_left[0:R, b, :]
                if s >= 2:
                    dve.wait_ge(split_step, s - 1)
                if part == 0:
                    ins = nc.vector.tensor_copy(
                        left.rearrange("g (o i p) -> g o i p", o=2, i=2),
                        t_rows[0:R, b, :].rearrange("g (p i o) -> g o i p", i=2, o=2))
                elif part % 2:
                    ins = nc.vector.tensor_copy(t_split[0:R, b, part // 2, :], left)
                else:
                    ins = nc.vector.tensor_tensor(left, left, t_split[0:R, b, part // 2 - 1, :], ALU.subtract)
                ins.then_inc(split_step, 1)

            dve.wait_ge(weights_in, 16 * N_WEIGHTS)
            for b, (t0, n) in enumerate(BLOCKS):
                if b < 12:
                    split_t(b)
                dve.wait_ge(table_ps, b + 1)
                if b >= 3:
                    dve.wait_ge(table_out[b % 3], b // 3 * 16)
                nc.vector.tensor_tensor(table_sb[:, b % 3, 0:n, :],
                                        banks[b % 2][0:NT, 0:n * C].rearrange("p (t c) -> p t c", c=C),
                                        bn1_all[0:NT, :].rearrange("p (a c) -> p a c", a=1).to_broadcast([NT, n, C]),
                                        ALU.add).then_inc(table_ready, 1)

            for b, bank in enumerate((psX, psA)):
                dve.wait_ge(ids_ps, b + 3)
                spread(dst_e, b, bank, dst_e_ready)
            dve.wait_ge(spans_in, 16)
            nc.vector.tensor_tensor(widths[:, :], spans[:, :, 1], spans[:, :, 0], ALU.subtract).then_inc(spans_ready, 1)
            dve.wait_ge(spans_ready, 1)
            nc.vector.tensor_reduce(widest[:, :], widths[:, :].rearrange("a (m g) -> a m g", g=SG), AX_X, ALU.max)\
                .then_inc(spans_ready, 1)
            dve.wait_ge(dst_e_ready, 2)
            dve.wait_ge(node_ids_ready, 1)
            dve.wait_ge(tables_zero, 2)
            dve.wait_ge(spans_ready, 2)

            windows = dve.alloc_register("dve_windows")
            dve.reg_mov(windows, 0)

            def find_hits(to, lo, g):
                return nc.vector.tensor_tensor(
                    to, node_ids[:, bass.ds(lo, W)].rearrange("p (a w) -> p a w", a=1).to_broadcast([P, TILES, W]),
                    dst_e[:, bass.ds(g, 1), :].rearrange("p a t -> p (a t)").rearrange("p (t a) -> p t a", a=1)
                    .to_broadcast([P, TILES, W]), ALU.is_equal)

            def add_tiles(to, hot):
                return nc.vector.tensor_reduce(to, hot.rearrange("p t w -> p w t"), AX_X, ALU.add)

            def add_at(to, lo, what):
                at = to[:, bass.ds(lo, W)]
                return nc.vector.tensor_tensor(at, at, what, ALU.add)

            def more_windows(m, g, counted):
                wide = nc.values_load(widest[0:1, bass.ds(m, 1)], engines=(DVE_ENGINE,), min_val=0, max_val=N - 1)
                with dve.If(wide >= W):
                    wait(dve, sums_added, g)
                    wait(dve, counts_added, counted)
                    for q in range(SG):
                        lo, hi = span_of(DVE_ENGINE, m * SG + q)
                        with dve.If(hi - lo >= W):
                            with dve.Fori(lo + W, hi + 1, W) as at:
                                dve.reg_add(windows, windows, 1)
                                n = dve.snap(windows, min_val=1)
                                find_hits(onehot_more[:, :, :], at, m * SG + q).then_inc(more_onehot, 1)
                                dve.wait_ge(more_onehot, n)
                                add_tiles(hits_more[:, :], onehot_more[:, :, :]).then_inc(more_hits, 1)
                                dve.wait_ge(more_hits, n)
                                add_at(counts, at, hits_more[:, :]).then_inc(more_counted, 1)
                                dve.wait_ge(more_sum, n)
                                add_at(sums, at, psA[:, 0:W]).then_inc(more_added, 1)
                                dve.wait_ge(more_counted, n)
                                dve.wait_ge(more_added, n)

            least = {}

            def step(i, k):
                if live(i, k, 3):
                    g = i * BODY + (k - 3)
                    least[(k - 3) % BODY] = lo = least_of(DVE_ENGINE, g)
                    wait(dve, sum_ps, g - 1)
                    find_hits(onehot[:, (k - 3) % 2, :, :], lo, g).then_inc(onehot_ready, 1)
                if live(i, k, 2):
                    g = i * BODY + (k - 2)
                    dve.wait_ge(ef_ps, g + 1)
                    dve.wait_ge(tw_ready, g + 1)
                    wait(dve, msg_ps, g - 1)
                    nc.vector.scalar_tensor_tensor(efw[:, (k - 2) % 2, :], psE[:, :], be2_c[:, :], tw[:, (k - 2) % 2, :],
                                                   ALU.add, ALU.mult).then_inc(efw_ready, 1)
                if live(i, k, 3):
                    g = i * BODY + (k - 3)
                    dve.wait_ge(onehot_ready, g + 1)
                    add_tiles(hits[:, (k - 3) % 2, :], onehot[:, (k - 3) % 2, :, :]).then_inc(hits_ready, 1)
                    dve.wait_ge(msg_ps, g + 1)
                    place = (k - 3) % BODY
                    dve.wait_ge(gather_in[place], (i if k < 3 else i + 1) * (16 * TILES))
                    wait(dve, h_ready, g - 1)
                    nc.vector.tensor_tensor(pre[:, (k - 3) % 2, :], psM[:, :], gathered[:, place, :], ALU.add)\
                        .then_inc(pre_ready, 1)
                    if place % SG == SG - 1 and not (isinstance(i, int) and i == TURNS):
                        stage_indices(i * 2 + (k - 3) // SG + 2, place // SG)
                    dve.wait_ge(hits_ready, g + 1)
                    wait(dve, counts_added, g)
                    add_at(counts, lo, hits[:, (k - 3) % 2, :]).then_inc(counts_added, 1)
                if live(i, k, 4):
                    g = i * BODY + (k - 4)
                    if k % SG == SG - 1:
                        last = isinstance(i, int) and i == TURNS
                        more_windows(i * 2 + (k - 4) // SG, g, G if last else g + 2)
                    lo = least_of(DVE_ENGINE, g) if k == 0 or (k - 4) % BODY not in least else least[(k - 4) % BODY]
                    dve.wait_ge(sum_ps, g + 1)
                    wait(dve, sums_added, g)
                    add_at(sums, lo, psA[:, 0:W]).then_inc(sums_added, 1)

            main_loop(dve, step, 4)

            def rescale(b):
                t0, n = BLOCKS[b]
                at = slice(t0, t0 + n)
                dve.wait_ge(std_ready, b + 1)
                nc.vector.reciprocal(rstd[:, at], std[:, at]).then_inc(rstd_ready, 1)
                dve.wait_ge(rstd_ready, b + 1)
                nc.vector.scalar_tensor_tensor(shift[:, at], mean_var[:, at, 0], -1.0, rstd[:, at], ALU.mult, ALU.mult)\
                    .then_inc(shift_ready, 1)

            for b, (t0, n) in enumerate(BLOCKS):
                rows = x_sb[:, t0:t0 + n, :]
                dve.wait_ge(y_ps, b + 1)
                nc.vector.scalar_tensor_tensor(rows, rows, 2.0,
                                               banks[b % 2][0:NT, 0:n * C].rearrange("p (t c) -> p t c", c=C),
                                               ALU.mult, ALU.add).then_inc(y_ready, 1)
                dve.wait_ge(y_ready, b + 1)
                for t in range(t0, t0 + n):
                    nc.vector.bn_stats(stats[:, t, :], x_sb[:, t, :]).then_inc(stats_ready, 1)
                for t in range(t0, t0 + n):
                    dve.wait_ge(stats_ready, t + 1)
                    nc.vector.bn_aggr(mean_var[:, t, :], stats[:, t, :]).then_inc(moments_ready, 1)
                if b >= 1:
                    rescale(b - 1)
            rescale(len(BLOCKS) - 1)


_INS = ['x', 'src', 'dst', 'edge_attr_64', 'edge_weight', 'L0_gnn_We1', 'L0_gnn_be1', 'L0_gnn_We2', 'L0_gnn_be2',
        'L0_gnn_Wt', 'L0_gnn_bt', 'L0_gnn_Wn1', 'L0_gnn_bn1', 'L0_gnn_Wn2', 'L0_gnn_bn2']
_OUT = ((6250, 128), 'float32')


def kernel(**inputs):
    import numpy as _np
    import concourse.bacc as _bacc
    from concourse import mybir as _mybir
    from concourse.bass_utils import run_bass_kernel_spmd as _run

    nc = _bacc.Bacc("TRN2", target_bir_lowering=False, num_devices=1)
    arrays, args = {}, []
    for name in _INS:
        a = _np.ascontiguousarray(inputs[name])
        arrays[f"in_{name}"] = a
        args.append(nc.dram_tensor(f"in_{name}", a.shape, _mybir.dt.from_np(a.dtype), kind="ExternalInput").ap())
    shape, dtype = _OUT
    args.append(nc.dram_tensor("out_y", shape, _mybir.dt.from_np(_np.dtype(dtype)), kind="ExternalOutput").ap())
    gnn_kernel(nc, *args)
    r = _run(nc, [arrays], core_ids=[0])
    return r.results[0]["out_y"]
```

```python
from contextlib import ExitStack

import concourse.bass as bass
from concourse import mybir

ALU = mybir.AluOpType
ACT = mybir.ActivationFunctionType
AX_X = mybir.AxisListType.X
F32 = mybir.dt.float32
BF16 = mybir.dt.bfloat16
I32 = mybir.dt.int32
DVE_ENGINE = mybir.EngineType.DVE
PE_ENGINE = mybir.EngineType.PE

P = 128
TILES = 4
GE = TILES * P
SG = 4
SE = SG * GE
W = 64
EPS = 1e-5
NT = 125
BT = 4
XCH = 10
PARTS = 3
ORDER = [0, 2, 1, 3]


def gnn_kernel(nc, x, src, dst, edge_attr, edge_weight, We1, be1, We2, be2, Wt, bt, Wn1, bn1, Wn2, bn2, out):
    N, C = x.shape
    E, F = edge_attr.shape
    SUPERS = 1 + E // SE
    G = SUPERS * SG
    SHARED = SUPERS * SE - E
    BODY = 2 * SG
    TURNS = SUPERS // 2
    RAW = BODY - 3
    EARLY = 2
    ROWS = [P, G - P]
    NTILES = N // NT
    BLOCKS = [(t, min(BT, NTILES - t)) for t in range(0, NTILES, BT)]
    CHUNKS = NTILES // XCH
    DOUBLINGS = next(n for n in range(16) if P << n >= N + W)
    ZERO = -(-(N + W) // len(BLOCKS))
    assert C == P and F == 64 and E % SE and SUPERS % 2 == 0 and P < G <= 2 * P
    assert N % NT == 0 and NTILES % XCH == 0 and 0 < SHARED <= GE

    table = nc.dram_tensor("node_table", (N, C), F32).ap()
    t_parts = nc.dram_tensor("t_parts", (PARTS, G, GE), BF16).ap()
    spans_dram = nc.dram_tensor("spans_dram", (G, 2), I32).ap()

    with ExitStack() as ctx:
        def sb(name, shape, dt=F32):
            return ctx.enter_context(nc.sbuf_tensor(name, shape, dt))

        def psum(name, shape):
            return ctx.enter_context(nc.psum_tensor(name, shape, F32))

        def sem(name):
            return ctx.enter_context(nc.semaphore(name))

        ident = sb("ident", [P, P])
        ones_parts = sb("ones_parts", [PARTS, P], BF16)
        node_ids = sb("node_ids", [P, N + W])
        we1 = sb("we1", [P, C])
        we2 = sb("we2", [P, C])
        wn1 = sb("wn1", [P, 2, C])
        wn2 = sb("wn2", [P, C])
        be1_c, be2_c, wt_c, bt_c = (sb(n, [P, 1]) for n in ("be1_c", "be2_c", "wt_c", "bt_c"))
        bn1_all = sb("bn1_all", [P, C])
        bn2_all = sb("bn2_all", [P, C])
        x_sb = sb("x_sb", [NT, NTILES, C])
        table_own = sb("table_own", [NT, 3, BT * C])
        sums = sb("sums", [P, N + W])
        counts = sb("counts", [P, N + W])
        zero_c = sb("zero_c", [P, 1])
        stats = sb("stats", [NT, NTILES, 6])
        mean_var = sb("mean_var", [NT, NTILES, 2])
        std, rstd, shift = (sb(n, [NT, NTILES]) for n in ("std", "rstd", "shift"))
        eps_c = sb("eps_c", [P, 1])
        src_rows = sb("src_rows", [P, 2, GE], I32)
        dst_rows = sb("dst_rows", [P, 2, GE], I32)
        t_split = sb("t_split", [P, 2, PARTS, GE], BF16)
        span_f = sb("span_f", [P, 2, 2])
        span_i = sb("span_i", [P, 2, 2], I32)
        src_e = sb("src_e", [P, G + BODY, TILES])
        dst_e = sb("dst_e", [P, G, TILES])
        spans = sb("spans", [1, G, 2], I32)
        widths = sb("widths", [1, G])
        widest = sb("widest", [1, SUPERS], I32)
        ea = [sb(f"ea{i}", [P, SG, TILES * F]) for i in range(2)]
        tp = [sb(f"tp{i}", [PARTS, SG, GE], BF16) for i in range(2)]
        idx = sb("idx", [P, BODY, TILES], I32)
        eaT = sb("eaT", [P, 2, 2, P])
        h1 = sb("h1", [P, 2, 2, GE // 2])
        tw = sb("tw", [P, 2, GE])
        efw = sb("efw", [P, 2, GE])
        gathered = sb("gathered", [P, BODY, GE])
        xgT = sb("xgT", [P, GE])
        pre = sb("pre", [P, 2, GE])
        h = sb("h", [P, BODY, GE])
        onehot = sb("onehot", [P, 2, TILES, W])
        onehot_more = sb("onehot_more", [P, TILES, W])
        hits = sb("hits", [P, 2, W])
        hits_more = sb("hits_more", [P, W])
        ids_f = h[:, 0:4, :].rearrange("p (a b) e -> p a b e", a=2)
        t_left = h[:, 4:6, :]
        t_rows = h[:, 6:8, :]
        table_sb = ([gathered[0:NT, place, :] for place in range(RAW, BODY)] + [pre[0:NT, b, :] for b in range(2)]
                    + [table_own[:, b, :] for b in range(3)])
        TB = len(table_sb)
        xT = efw[:, :, :].rearrange("p b (t n) -> p b t n", t=BT)

        psT = psum("psT", [P, 2, P])
        psH = psum("psH", [P, 2, 512])
        psB = psum("psB", [P, GE])
        psE = psum("psE", [P, GE])
        psM = psum("psM", [P, GE])
        psA = psum("psA", [P, 512])
        psX = psum("psX", [P, 512])
        xT_banks, table_banks = [psX, psE], [psM, psA]
        y_banks = [psE, psM]

        wn1_in, weights_in, dst_in, t_in = (sem(n) for n in ("wn1_in", "weights_in", "dst_in", "t_in"))
        src_in = [sem(f"src_in{b}") for b in range(2)]
        x_in = [sem(f"x_in{i}") for i in range(CHUNKS)]
        table_out = [sem(f"table_out{i}") for i in range(TB)]
        t_out, span_out, spans_in = sem("t_out"), sem("span_out"), sem("spans_in")
        ea_in = [sem(f"ea_in{i}") for i in range(2)]
        tp_in = [sem(f"tp_in{i}") for i in range(2)]
        gather_in = [sem(f"gather_in{i}") for i in range(BODY)]
        y_out = sem("y_out")
        ident_ready, ones_ready, node_ids_ready, tables_zero = (
            sem(n) for n in ("ident_ready", "ones_ready", "node_ids_ready", "tables_zero"))
        xg_ps, xgT_ready = sem("xg_ps"), sem("xgT_ready")
        xT_ps, xT_ready, table_ps, table_ready = (sem(n) for n in ("xT_ps", "xT_ready", "table_ps", "table_ready"))
        src_cast, dst_cast, dst_masked = sem("src_cast"), sem("dst_cast"), sem("dst_masked")
        ids_ps, src_e_ready, dst_e_ready = sem("ids_ps"), sem("src_e_ready"), sem("dst_e_ready")
        split_step, span_found, span_ready, spans_ready = (
            sem(n) for n in ("split_step", "span_found", "span_ready", "spans_ready"))
        idx_ready = sem("idx_ready")
        eaT_ps, eaT_ready, h1_ps, h1_ready = (sem(n) for n in ("eaT_ps", "eaT_ready", "h1_ps", "h1_ready"))
        t_ps, tw_ready, ef_ps, efw_ready = (sem(n) for n in ("t_ps", "tw_ready", "ef_ps", "efw_ready"))
        msg_ps, pre_ready, h_ready = (sem(n) for n in ("msg_ps", "pre_ready", "h_ready"))
        onehot_ready, hits_ready, counts_added = (sem(n) for n in ("onehot_ready", "hits_ready", "counts_added"))
        sum_ps, sums_added = sem("sum_ps"), sem("sums_added")
        more_onehot, more_hits, more_counted, more_sum, more_added = (
            sem(n) for n in ("more_onehot", "more_hits", "more_counted", "more_sum", "more_added"))
        y_ps, y_ready, stats_ready, moments_ready = (sem(n) for n in ("y_ps", "y_ready", "stats_ready", "moments_ready"))
        std_ready, rstd_ready, shift_ready, y_done = (sem(n) for n in ("std_ready", "rstd_ready", "shift_ready", "y_done"))

        block = ctx.enter_context(nc.Block())

        x_tiles = x.rearrange("(t n) c -> n t c", n=NT)
        out_tiles = out.rearrange("(t n) c -> n t c", n=NT)
        table_tiles = table.rearrange("(t n) c -> n t c", n=NT)

        def wait(eng, semaphore, value):
            if not (isinstance(value, int) and value <= 0):
                eng.wait_ge(semaphore, value)

        def wait_table(eng):
            for r in range(TB):
                eng.wait_ge(table_out[r], 16 * len(BLOCKS[r::TB]))

        def live(i, k, lag):
            return not isinstance(i, int) or (k >= lag if i == 0 else k < lag)

        def raw(i, g):
            return isinstance(i, int) and i == 0 and 0 <= g < RAW

        def main_loop(eng, step, depth):
            for k in range(EARLY, BODY):
                step(0, k)
            with eng.Fori(1, TURNS) as i:
                for k in range(BODY):
                    step(i, k)
            for k in range(depth):
                step(TURNS, k)

        def span_of(engine, g):
            return (nc.values_load(spans[0:1, bass.ds(g, 1), 0], engines=(engine,), min_val=0, max_val=N - 1),
                    nc.values_load(spans[0:1, bass.ds(g, 1), 1], engines=(engine,), min_val=0, max_val=N - 1))

        def least_of(engine, g):
            return nc.values_load(spans[0:1, bass.ds(g, 1), 0], engines=(engine,), min_val=0, max_val=N - 1)

        def by_group(a):
            return [a[E - SE:E].rearrange("(g e) -> g e", e=GE),
                    a[0:(P - SG) * GE].rearrange("(g e) -> g e", e=GE),
                    a[(P - SG) * GE:(G - SG) * GE].rearrange("(g e) -> g e", e=GE)]

        col, row = "(c a) -> c a", "(a c) -> a c"
        loads_first = [(wn1[:, :, :], Wn1.rearrange("(a k) c -> k a c", k=P)),
                       (bn1_all[:, :], bn1.rearrange(row, a=1).to_broadcast([P, C]))]
        loads_act = [(we1[0:F, :], We1), (we1[F:2 * F, :], We1), (be1_c[:, :], be1.rearrange(col, a=1)),
                     (we2[:, :], We2)]
        loads_sp = [(bt_c[:, :], bt.rearrange(col, a=1)), (wt_c[:, :], Wt.rearrange("a c -> c a")),
                    (be2_c[:, :], be2.rearrange(col, a=1)), (wn2[:, :], Wn2),
                    (bn2_all[:, :], bn2.rearrange(row, a=1).to_broadcast([P, C]))]
        N_WEIGHTS = len(loads_act) + len(loads_sp)

        @block.sync
        def _(sp):
            def load_x(c):
                sp.dma_start(x_sb[:, c * XCH:(c + 1) * XCH, :],
                             x_tiles[:, c * XCH:(c + 1) * XCH, :]).then_inc(x_in[c], 16)

            def load_rows(tile, a, landed, parts=(0, 1, 2)):
                last, first, second = by_group(a)
                places = [(tile[0:SG, 0, :], last), (tile[SG:P, 0, :], first), (tile[0:ROWS[1], 1, :], second)]
                for n in parts:
                    sp.dma_start(*places[n]).then_inc(landed, 16)

            load_rows(src_rows, src, src_in[0], (0, 1))
            load_x(0)
            load_rows(src_rows, src, src_in[1], (2,))
            load_rows(dst_rows, dst, dst_in)
            load_x(1)
            load_rows(t_rows, edge_weight, t_in)
            load_x(2)
            for c in range(3, CHUNKS):
                load_x(c)
            for to, of in loads_sp:
                sp.dma_start(to, of).then_inc(weights_in, 16)

            def load_edges(slot, start):
                sp.dma_start(ea[slot][:, :, :],
                             edge_attr[bass.ds(start, SE), :].rearrange("(g p j) f -> p g (j f)", p=P, j=TILES))\
                    .then_inc(ea_in[slot], 16)

            def load_t(m, slot):
                sp.dma_start(tp[slot][:, :, :], t_parts[:, bass.ds(m * SG, SG), :]).then_inc(tp_in[slot], 16)

            load_edges(0, E - SE)

            def store_parts(r):
                sp.wait_ge(split_step, 6 * r + 6)
                sp.dma_start(t_parts[:, r * P:r * P + ROWS[r], :].rearrange("k g e -> g k e"),
                             t_split[0:ROWS[r], r, :, :]).then_inc(t_out, 16)

            for b, (t0, n) in enumerate(BLOCKS):
                sp.wait_ge(table_ready, b + 1)
                sp.dma_start(table_tiles[:, t0:t0 + n, :], table_sb[b % TB][:, 0:n * C].rearrange("p (t c) -> p t c", c=C))\
                    .then_inc(table_out[b % TB], 16)
                if b == 2:
                    sp.wait_ge(span_ready, 2)
                    for r in range(2):
                        sp.dma_start(spans_dram[r * P:r * P + ROWS[r], :], span_i[0:ROWS[r], r, :])\
                            .then_inc(span_out, 16)
                if b == 5:
                    sp.wait_ge(span_out, 32)
                    sp.dma_start(spans[:, :, :], spans_dram.rearrange("(a g) k -> a g k", a=1)).then_inc(spans_in, 16)
                if b == 6:
                    store_parts(0)
                if b == 9:
                    sp.wait_ge(t_out, 16)
                    load_t(0, 0)

            load_edges(1, 0)
            load_t(1, 1)
            store_parts(1)
            sp.wait_ge(t_out, 32)

            def load_super(m, slot, start):
                sp.wait_ge(eaT_ps, (m - 1) * SG)
                sp.wait_ge(t_ps, (m - 1) * SG)
                load_edges(slot, start)
                load_t(m, slot)

            with sp.Fori(1, TURNS) as i:
                load_super(i * 2, 0, i * (2 * SE) - SE)
                load_super(i * 2 + 1, 1, i * (2 * SE))

            for c in range(CHUNKS):
                sp.wait_ge(y_done, (c + 1) * XCH)
                sp.dma_start(out_tiles[:, c * XCH:(c + 1) * XCH, :],
                             x_sb[:, c * XCH:(c + 1) * XCH, :]).then_inc(y_out, 16)
            sp.wait_ge(y_out, 16 * CHUNKS)

        @block.gpsimd
        def _(pool):
            pool.memset(ident[:, :], 0.0).then_inc(ident_ready, 1)
            pool.wait_ge(ident_ready, 1)
            pool.affine_select(out=ident[:, :], in_=ident[:, :], compare_op=ALU.not_equal, fill=1.0,
                               base=0, pattern=[[-1, P]], channel_multiplier=1).then_inc(ident_ready, 1)
            pool.iota(node_ids[:, 0:P], pattern=[[1, P]], base=0, channel_multiplier=0,
                      allow_small_or_imprecise_dtypes=True).then_inc(node_ids_ready, 1)
            pool.memset(ones_parts[:, :], 1.0).then_inc(ones_ready, 1)
            pool.memset(eps_c[:, :], EPS).then_inc(ones_ready, 1)
            pool.memset(zero_c[:, :], 0.0).then_inc(ones_ready, 1)
            pool.memset(sums[:, :], 0.0).then_inc(tables_zero, 1)

            def gather_group(place, rows):
                for t in range(TILES):
                    pool.indirect_dma_start(
                        gathered[:, place, t * C:(t + 1) * C], None, rows,
                        bass.IndirectOffsetOnAxis(idx[:, place, t:t + 1], 0)).then_inc(gather_in[place], 16)

            pool.wait_ge(idx_ready, BODY)
            for place in range(BODY):
                if place == RAW:
                    wait_table(pool)
                gather_group(place, x if place < RAW else table)

            with pool.Fori(1, TURNS) as i:
                for place in range(BODY):
                    g = i * BODY + place
                    pool.wait_ge(pre_ready, g - (BODY - 1))
                    pool.nop(nofuse=True)
                    pool.wait_ge(idx_ready, g + 1)
                    pool.nop(nofuse=True)
                    gather_group(place, table)

        @block.scalar
        def _(act):
            for to, of in loads_first:
                act.dma_start(to, of).then_inc(wn1_in, 16)
            for to, of in loads_act:
                act.dma_start(to, of).then_inc(weights_in, 16)

            act.wait_ge(ones_ready, 3)
            nc.scalar.activation(std[:, 0:1], zero_c[0:NT, :], ACT.Sigmoid)

            def zero_counts(b):
                at = slice(b * ZERO, min(N + W, (b + 1) * ZERO))
                nc.scalar.activation(counts[:, at], zero_c[:, :].to_broadcast([P, at.stop - at.start]), ACT.Copy)\
                    .then_inc(tables_zero, 1)

            def step(i, k):
                if live(i, k, 0) and not (isinstance(i, int) and i == TURNS):
                    g = i * BODY + k
                    act.wait_ge(eaT_ps, g + 1)
                    wait(act, h1_ps, g - 1)
                    nc.scalar.activation(eaT[:, k % 2, :, :], psT[:, :, :], ACT.Copy).then_inc(eaT_ready, 1)
                if live(i, k, 1):
                    g = i * BODY + (k - 1)
                    act.wait_ge(h1_ps, g + 1)
                    wait(act, ef_ps, g - 1)
                    nc.scalar.activation(h1[:, (k - 1) % 2, :, :], psH[:, :, 0:GE // 2], ACT.Relu,
                                         bias=be1_c[:, :]).then_inc(h1_ready, 1)
                    act.wait_ge(t_ps, g + 1)
                    wait(act, efw_ready, g - 1)
                    nc.scalar.activation(tw[:, (k - 1) % 2, :], psB[:, :], ACT.Sigmoid, bias=bt_c[:, :],
                                         scale=wt_c[:, :]).then_inc(tw_ready, 1)
                if raw(i, k - 2):
                    act.wait_ge(xg_ps, k - 1)
                    wait(act, msg_ps, k - 2)
                    nc.scalar.activation(xgT[:, :], psX[:, :], ACT.Copy).then_inc(xgT_ready, 1)
                if live(i, k, 3):
                    g = i * BODY + (k - 3)
                    act.wait_ge(pre_ready, g + 1)
                    if (k - 3) % SG == 0:
                        wait(act, sum_ps, g - SG)
                    nc.scalar.activation(h[:, (k - 3) % BODY, :], pre[:, (k - 3) % 2, :], ACT.Relu).then_inc(h_ready, 1)

            for b, (t0, n) in enumerate(BLOCKS):
                act.wait_ge(xT_ps, b + 1)
                if b >= 2:
                    act.wait_ge(table_ps, b - 1)
                nc.scalar.activation(xT[:, b % 2, 0:n, 0:NT],
                                     xT_banks[b % 2][:, :].rearrange("p (t n) -> p t n", t=BT)[:, 0:n, 0:NT],
                                     ACT.Copy).then_inc(xT_ready, 1)
                zero_counts(b)


            act.wait_ge(weights_in, 16 * N_WEIGHTS)
            for k in range(EARLY):
                step(0, k)

            act.wait_ge(split_step, 12)
            act.wait_ge(ids_ps, 4)
            main_loop(act, step, 3)

            def normalize(b):
                t0, n = BLOCKS[b]
                act.wait_ge(shift_ready, b + 1)
                for t in range(t0, t0 + n):
                    nc.scalar.activation(x_sb[:, t, :], x_sb[:, t, :], ACT.Identity, bias=shift[:, t:t + 1],
                                         scale=rstd[:, t:t + 1]).then_inc(y_done, 1)

            act.wait_ge(ones_ready, 2)
            for b, (t0, n) in enumerate(BLOCKS):
                act.wait_ge(moments_ready, (t0 + n))
                nc.scalar.activation(std[:, t0:t0 + n], mean_var[:, t0:t0 + n, 1], ACT.Sqrt,
                                     bias=eps_c[0:NT, :]).then_inc(std_ready, 1)
                if b >= 1:
                    normalize(b - 1)
            normalize(len(BLOCKS) - 1)

        @block.tensor
        def _(pe):
            def transpose_ids(a, b):
                rows = ids_f[0:ROWS[b], a, b, :].rearrange("g (p j) -> g j p", j=TILES)
                for q, j in enumerate(ORDER):
                    mm = nc.tensor.transpose(psH[:, b, q * P:q * P + ROWS[b]], rows[:, j, :],
                                             ident[0:ROWS[b], 0:ROWS[b]])
                mm.then_inc(ids_ps, 1)

            pe.wait_ge(ident_ready, 2)
            pe.wait_ge(src_cast, 1)
            transpose_ids(0, 0)

            def transpose_x(b):
                t0, n = BLOCKS[b]
                for c in range(t0 // XCH, (t0 + n - 1) // XCH + 1):
                    pe.wait_ge(x_in[c], 16)
                if b >= 2:
                    pe.wait_ge(xT_ready, b - 1)
                for q in range(n):
                    mm = nc.tensor.transpose(xT_banks[b % 2][:, q * P:q * P + NT], x_sb[:, t0 + q, :],
                                             ident[0:NT, 0:NT])
                mm.then_inc(xT_ps, 1)

            def multiply_x(b):
                t0, n = BLOCKS[b]
                pe.wait_ge(xT_ready, b + 1)
                if b >= 2:
                    pe.wait_ge(table_ready, b - 1)
                for q in range(n):
                    mm = nc.tensor.matmul(table_banks[b % 2][0:NT, q * P:(q + 1) * P], xT[:, b % 2, q, 0:NT], wn1[:, 0, :],
                                          start=True, stop=True)
                mm.then_inc(table_ps, 1)

            windows = pe.alloc_register("pe_windows")
            pe.reg_mov(windows, 0)

            def more_windows(m, g, place):
                if isinstance(m, int) and m == 0:
                    pe.wait_ge(spans_ready, 2)
                wide = nc.values_load(widest[0:1, bass.ds(m, 1)], engines=(PE_ENGINE,), min_val=0, max_val=N - 1)
                with pe.If(wide >= W):
                    wait(pe, sums_added, g)
                    for q in range(SG):
                        lo, hi = span_of(PE_ENGINE, m * SG + q)
                        with pe.If(hi - lo >= W):
                            with pe.Fori(lo + W, hi + 1, W):
                                pe.reg_add(windows, windows, 1)
                                n = pe.snap(windows, min_val=1)
                                pe.wait_ge(more_onehot, n)
                                for t in range(TILES):
                                    mm = nc.tensor.matmul(psA[:, 0:W], h[:, place + q, t * C:(t + 1) * C],
                                                          onehot_more[:, t, :], start=(t == 0), stop=(t == TILES - 1))
                                mm.then_inc(more_sum, 1)
                                pe.wait_ge(more_added, n)

            def step(i, k):
                if live(i, k, 0) and not (isinstance(i, int) and i == TURNS):
                    g = i * BODY + k
                    if k % SG == 0:
                        pe.wait_ge(ea_in[k // SG], i * 16 + 16)
                    wait(pe, eaT_ready, g)
                    for a in range(2):
                        mm = nc.tensor.transpose(psT[:, a, :], ea[k // SG][:, k % SG, a * P:(a + 1) * P], ident[:, :])
                    mm.then_inc(eaT_ps, 1)
                if live(i, k, 1):
                    g = i * BODY + (k - 1)
                    pe.wait_ge(eaT_ready, g + 1)
                    wait(pe, h1_ready, g)
                    for a in range(2):
                        mm = nc.tensor.matmul(psH[:, a, 0:GE // 2], we1[a * F:(a + 1) * F, :],
                                              eaT[a * F:(a + 1) * F, (k - 1) % 2, :, :], start=True, stop=True)
                    mm.then_inc(h1_ps, 1)
                    if (k - 1) % SG == 0:
                        pe.wait_ge(tp_in[(k - 1) // SG % 2], i * 16 + 16)
                    wait(pe, tw_ready, g)
                    nc.tensor.matmul(psB[:, :], ones_parts[:, :], tp[(k - 1) // SG % 2][:, (k - 1) % SG, :],
                                     start=True, stop=True).then_inc(t_ps, 1)
                if live(i, k, 2):
                    g = i * BODY + (k - 2)
                    pe.wait_ge(h1_ready, g + 1)
                    wait(pe, efw_ready, g)
                    nc.tensor.matmul(psE[:, :], we2[:, :], h1[:, (k - 2) % 2, :, :], start=True, stop=True)\
                        .then_inc(ef_ps, 1)
                if raw(i, k - 2):
                    place = k - 2
                    pe.wait_ge(gather_in[place], 16 * TILES)
                    wait(pe, xgT_ready, place)
                    for t in range(TILES):
                        mm = nc.tensor.transpose(psX[:, t * P:(t + 1) * P], gathered[:, place, t * C:(t + 1) * C],
                                                 ident[:, :])
                    mm.then_inc(xg_ps, 1)
                if live(i, k, 3):
                    g = i * BODY + (k - 3)
                    pe.wait_ge(efw_ready, g + 1)
                    wait(pe, pre_ready, g)
                    if raw(i, k - 3):
                        pe.wait_ge(xgT_ready, k - 2)
                    for t in range(TILES):
                        at = slice(t * P, (t + 1) * P)
                        mm = nc.tensor.matmul(psM[:, at], efw[:, (k - 3) % 2, at], wn1[:, 1, :],
                                              start=True, stop=not raw(i, k - 3))
                        if raw(i, k - 3):
                            mm = nc.tensor.matmul(psM[:, at], xgT[:, at], wn1[:, 0, :], start=False, stop=True)
                    mm.then_inc(msg_ps, 1)
                if live(i, k, 4):
                    g = i * BODY + (k - 4)
                    pe.wait_ge(h_ready, g + 1)
                    if k % SG == SG - 1:
                        more_windows(i * 2 + (k - 4) // SG, g, (k - 4) // SG % 2 * SG)
                    pe.wait_ge(onehot_ready, g + 1)
                    wait(pe, sums_added, g)
                    for t in range(TILES):
                        mm = nc.tensor.matmul(psA[:, 0:W], h[:, (k - 4) % BODY, t * C:(t + 1) * C],
                                              onehot[:, (k - 4) % 2, t, :], start=(t == 0), stop=(t == TILES - 1))
                    mm.then_inc(sum_ps, 1)

            pe.wait_ge(src_cast, 2)
            transpose_ids(0, 1)
            transpose_x(0)
            pe.wait_ge(wn1_in, 32)
            for b in range(len(BLOCKS)):
                if b + 1 < len(BLOCKS):
                    transpose_x(b + 1)
                multiply_x(b)
                if b == 3:
                    pe.wait_ge(dst_masked, 1)
                    for r in range(2):
                        pe.wait_ge(src_e_ready, r + 1)
                        transpose_ids(1, r)
                if b == len(BLOCKS) - EARLY:
                    pe.wait_ge(weights_in, 16 * N_WEIGHTS)
                    pe.wait_ge(dst_e_ready, 2)
                    pe.wait_ge(ones_ready, 1)
                if b >= len(BLOCKS) - EARLY:
                    step(0, b - (len(BLOCKS) - EARLY))

            pe.wait_ge(xT_ready, len(BLOCKS))
            pe.wait_ge(table_ready, len(BLOCKS))
            main_loop(pe, step, 4)

            pe.wait_ge(sums_added, G)
            pe.wait_ge(counts_added, G)
            for b, (t0, n) in enumerate(BLOCKS):
                if b >= 2:
                    pe.wait_ge(y_ready, b - 1)
                for q in range(n):
                    at = slice((t0 + q) * NT, (t0 + q + 1) * NT)
                    rows = y_banks[b % 2][0:NT, q * P:(q + 1) * P]
                    nc.tensor.matmul(rows, sums[:, at], wn2[:, :], start=True, stop=False)
                    mm = nc.tensor.matmul(rows, counts[:, at], bn2_all[:, :], start=False, stop=True)
                mm.then_inc(y_ps, 1)

        @block.vector
        def _(dve):
            def cast(a, rows, b, done):
                nc.vector.tensor_copy(ids_f[0:ROWS[b], a, b, :], rows[0:ROWS[b], b, :]).then_inc(done, 1)

            def spread(ids, b, ready):
                nc.vector.tensor_copy(ids[:, b * P:b * P + ROWS[b], :].rearrange("p g q -> p q g"),
                                      psH[:, b, :].rearrange("p (q g) -> p q g", q=TILES)[:, :, 0:ROWS[b]])\
                    .then_inc(ready, 1)

            def stage_indices(g, place, n):
                nc.vector.tensor_copy(idx[:, place:place + n, :], src_e[:, bass.ds(g, n), :]).then_inc(idx_ready, n)

            def double_ids(n):
                have = P << n
                more = min(have, N + W - have)
                dve.wait_ge(node_ids_ready, 1 + n)
                nc.vector.tensor_scalar(node_ids[:, have:have + more], node_ids[:, 0:more], float(have), None, ALU.add)\
                    .then_inc(node_ids_ready, 1)

            for n in range(DOUBLINGS - 1):
                double_ids(n)

            nc.vector.memset(src_e[:, G:G + BODY, :], 0.0)
            dve.wait_ge(src_in[0], 32)
            cast(0, src_rows, 0, src_cast)
            dve.wait_ge(ids_ps, 1)
            spread(src_e, 0, src_e_ready)
            dve.wait_ge(src_e_ready, 1)
            stage_indices(0, 0, BODY)
            dve.wait_ge(src_in[1], 16)
            cast(0, src_rows, 1, src_cast)
            dve.wait_ge(ids_ps, 2)
            spread(src_e, 1, src_e_ready)

            dve.wait_ge(dst_in, 48)
            for b in range(2):
                cast(1, dst_rows, b, dst_cast)
            dve.wait_ge(dst_cast, 2)
            double_ids(DOUBLINGS - 1)

            def find_spans(b):
                for n, op in enumerate((ALU.min, ALU.max)):
                    nc.vector.tensor_reduce(span_f[0:ROWS[b], b, n:n + 1], ids_f[0:ROWS[b], 1, b, :], AX_X, op)\
                        .then_inc(span_found, 1)

            def split_t(s):
                b, part = s // 6, s % 6
                R = ROWS[b]
                left = t_left[0:R, b, :]
                if part > 0:
                    dve.wait_ge(split_step, s)
                if part == 0:
                    ins = nc.vector.tensor_copy(
                        left.rearrange("g (o i p) -> g o i p", o=2, i=2),
                        t_rows[0:R, b, :].rearrange("g (p i o) -> g o i p", i=2, o=2))
                elif part % 2:
                    ins = nc.vector.tensor_copy(t_split[0:R, b, part // 2, :], left)
                else:
                    ins = nc.vector.tensor_tensor(left, left, t_split[0:R, b, part // 2 - 1, :], ALU.subtract)
                ins.then_inc(split_step, 1)

            dve.wait_ge(wn1_in, 32)
            for b, (t0, n) in enumerate(BLOCKS):
                dve.wait_ge(table_ps, b + 1)
                if b >= TB:
                    dve.wait_ge(table_out[b % TB], b // TB * 16)
                nc.vector.tensor_tensor(table_sb[b % TB][:, 0:n * C].rearrange("p (t c) -> p t c", c=C),
                                        table_banks[b % 2][0:NT, 0:n * C].rearrange("p (t c) -> p t c", c=C),
                                        bn1_all[0:NT, :].rearrange("p (a c) -> p a c", a=1).to_broadcast([NT, n, C]),
                                        ALU.add).then_inc(table_ready, 1)
                if b == 0:
                    find_spans(0)
                    dve.wait_ge(span_found, 2)
                    nc.vector.memset(ids_f[0:1, 1, 0, 0:SHARED], -1.0).then_inc(dst_masked, 1)
                if b == 1:
                    find_spans(1)
                if b == 2:
                    dve.wait_ge(span_found, 4)
                    for r in range(2):
                        nc.vector.tensor_copy(span_i[0:ROWS[r], r, :], span_f[0:ROWS[r], r, :]).then_inc(span_ready, 1)
                    dve.wait_ge(t_in, 48)
                    split_t(0)
                if b >= 2:
                    split_t(b - 1)
                if b == 6:
                    for r in range(2):
                        dve.wait_ge(ids_ps, 3 + r)
                        spread(dst_e, r, dst_e_ready)
            dve.wait_ge(spans_in, 16)
            nc.vector.tensor_tensor(widths[:, :], spans[:, :, 1], spans[:, :, 0], ALU.subtract).then_inc(spans_ready, 1)
            dve.wait_ge(spans_ready, 1)
            nc.vector.tensor_reduce(widest[:, :], widths[:, :].rearrange("a (m g) -> a m g", g=SG), AX_X, ALU.max)\
                .then_inc(spans_ready, 1)
            dve.wait_ge(node_ids_ready, 1 + DOUBLINGS)
            dve.wait_ge(dst_e_ready, 2)
            dve.wait_ge(weights_in, 16 * N_WEIGHTS)
            dve.wait_ge(tables_zero, 1 + len(BLOCKS))
            dve.wait_ge(spans_ready, 2)

            windows = dve.alloc_register("dve_windows")
            dve.reg_mov(windows, 0)

            def find_hits(to, lo, g):
                return nc.vector.tensor_tensor(
                    to, node_ids[:, bass.ds(lo, W)].rearrange("p (a w) -> p a w", a=1).to_broadcast([P, TILES, W]),
                    dst_e[:, bass.ds(g, 1), :].rearrange("p a t -> p (a t)").rearrange("p (t a) -> p t a", a=1)
                    .to_broadcast([P, TILES, W]), ALU.is_equal)

            def add_tiles(to, hot):
                return nc.vector.tensor_reduce(to, hot.rearrange("p t w -> p w t"), AX_X, ALU.add)

            def add_at(to, lo, what):
                at = to[:, bass.ds(lo, W)]
                return nc.vector.tensor_tensor(at, at, what, ALU.add)

            def more_windows(m, g, counted):
                wide = nc.values_load(widest[0:1, bass.ds(m, 1)], engines=(DVE_ENGINE,), min_val=0, max_val=N - 1)
                with dve.If(wide >= W):
                    wait(dve, sums_added, g)
                    wait(dve, counts_added, counted)
                    for q in range(SG):
                        lo, hi = span_of(DVE_ENGINE, m * SG + q)
                        with dve.If(hi - lo >= W):
                            with dve.Fori(lo + W, hi + 1, W) as at:
                                dve.reg_add(windows, windows, 1)
                                n = dve.snap(windows, min_val=1)
                                find_hits(onehot_more[:, :, :], at, m * SG + q).then_inc(more_onehot, 1)
                                dve.wait_ge(more_onehot, n)
                                add_tiles(hits_more[:, :], onehot_more[:, :, :]).then_inc(more_hits, 1)
                                dve.wait_ge(more_hits, n)
                                add_at(counts, at, hits_more[:, :]).then_inc(more_counted, 1)
                                dve.wait_ge(more_sum, n)
                                add_at(sums, at, psA[:, 0:W]).then_inc(more_added, 1)
                                dve.wait_ge(more_counted, n)
                                dve.wait_ge(more_added, n)

            least = {}

            def step(i, k):
                if live(i, k, 3):
                    g = i * BODY + (k - 3)
                    least[(k - 3) % BODY] = lo = least_of(DVE_ENGINE, g)
                    wait(dve, sum_ps, g - 1)
                    find_hits(onehot[:, (k - 3) % 2, :, :], lo, g).then_inc(onehot_ready, 1)
                if live(i, k, 2):
                    g = i * BODY + (k - 2)
                    dve.wait_ge(ef_ps, g + 1)
                    dve.wait_ge(tw_ready, g + 1)
                    wait(dve, msg_ps, g - 1)
                    nc.vector.scalar_tensor_tensor(efw[:, (k - 2) % 2, :], psE[:, :], be2_c[:, :], tw[:, (k - 2) % 2, :],
                                                   ALU.add, ALU.mult).then_inc(efw_ready, 1)
                if live(i, k, 3):
                    g = i * BODY + (k - 3)
                    dve.wait_ge(onehot_ready, g + 1)
                    add_tiles(hits[:, (k - 3) % 2, :], onehot[:, (k - 3) % 2, :, :]).then_inc(hits_ready, 1)
                    dve.wait_ge(msg_ps, g + 1)
                    place = (k - 3) % BODY
                    dve.wait_ge(gather_in[place], (i if k < 3 else i + 1) * (16 * TILES))
                    wait(dve, h_ready, g - 1)
                    if isinstance(i, int) and i == 0 and k == 3:
                        wait_table(dve)
                    tiled = "p (t c) -> p t c"
                    if raw(i, k - 3):
                        rest = bn1_all[:, :].rearrange("p (a c) -> p a c", a=1).to_broadcast([P, TILES, C])
                    else:
                        rest = gathered[:, place, :].rearrange(tiled, c=C)
                    nc.vector.tensor_tensor(pre[:, (k - 3) % 2, :].rearrange(tiled, c=C),
                                            psM[:, :].rearrange(tiled, c=C), rest, ALU.add).then_inc(pre_ready, 1)
                    if not (isinstance(i, int) and i == TURNS):
                        stage_indices(g + BODY, place, 1)
                    dve.wait_ge(hits_ready, g + 1)
                    wait(dve, counts_added, g)
                    add_at(counts, lo, hits[:, (k - 3) % 2, :]).then_inc(counts_added, 1)
                if live(i, k, 4):
                    g = i * BODY + (k - 4)
                    if k % SG == SG - 1:
                        last = isinstance(i, int) and i == TURNS
                        more_windows(i * 2 + (k - 4) // SG, g, G if last else g + 2)
                    lo = least_of(DVE_ENGINE, g) if k == 0 or (k - 4) % BODY not in least else least[(k - 4) % BODY]
                    dve.wait_ge(sum_ps, g + 1)
                    wait(dve, sums_added, g)
                    add_at(sums, lo, psA[:, 0:W]).then_inc(sums_added, 1)

            main_loop(dve, step, 4)

            def rescale(b):
                t0, n = BLOCKS[b]
                at = slice(t0, t0 + n)
                dve.wait_ge(std_ready, b + 1)
                nc.vector.reciprocal(rstd[:, at], std[:, at]).then_inc(rstd_ready, 1)
                dve.wait_ge(rstd_ready, b + 1)
                nc.vector.scalar_tensor_tensor(shift[:, at], mean_var[:, at, 0], -1.0, rstd[:, at], ALU.mult, ALU.mult)\
                    .then_inc(shift_ready, 1)

            for b, (t0, n) in enumerate(BLOCKS):
                rows = x_sb[:, t0:t0 + n, :]
                dve.wait_ge(y_ps, b + 1)
                nc.vector.scalar_tensor_tensor(rows, rows, 2.0,
                                               y_banks[b % 2][0:NT, 0:n * C].rearrange("p (t c) -> p t c", c=C),
                                               ALU.mult, ALU.add).then_inc(y_ready, 1)
                dve.wait_ge(y_ready, b + 1)
                for t in range(t0, t0 + n):
                    nc.vector.bn_stats(stats[:, t, :], x_sb[:, t, :]).then_inc(stats_ready, 1)
                for t in range(t0, t0 + n):
                    dve.wait_ge(stats_ready, t + 1)
                    nc.vector.bn_aggr(mean_var[:, t, :], stats[:, t, :]).then_inc(moments_ready, 1)
                if b >= 1:
                    rescale(b - 1)
            rescale(len(BLOCKS) - 1)


_INS = ['x', 'src', 'dst', 'edge_attr_64', 'edge_weight', 'L0_gnn_We1', 'L0_gnn_be1', 'L0_gnn_We2', 'L0_gnn_be2',
        'L0_gnn_Wt', 'L0_gnn_bt', 'L0_gnn_Wn1', 'L0_gnn_bn1', 'L0_gnn_Wn2', 'L0_gnn_bn2']
_OUT = ((6250, 128), 'float32')


def kernel(**inputs):
    import numpy as _np
    import concourse.bacc as _bacc
    from concourse import mybir as _mybir
    from concourse.bass_utils import run_bass_kernel_spmd as _run

    nc = _bacc.Bacc("TRN2", target_bir_lowering=False, num_devices=1)
    arrays, args = {}, []
    for name in _INS:
        a = _np.ascontiguousarray(inputs[name])
        arrays[f"in_{name}"] = a
        args.append(nc.dram_tensor(f"in_{name}", a.shape, _mybir.dt.from_np(a.dtype), kind="ExternalInput").ap())
    shape, dtype = _OUT
    args.append(nc.dram_tensor("out_y", shape, _mybir.dt.from_np(_np.dtype(dtype)), kind="ExternalOutput").ap())
    gnn_kernel(nc, *args)
    r = _run(nc, [arrays], core_ids=[0])
    return r.results[0]["out_y"]
```

```python
from contextlib import ExitStack

import concourse.bass as bass
from concourse import mybir

ALU = mybir.AluOpType
ACT = mybir.ActivationFunctionType
AX_X = mybir.AxisListType.X
F32 = mybir.dt.float32
BF16 = mybir.dt.bfloat16
I32 = mybir.dt.int32
DVE_ENGINE = mybir.EngineType.DVE
PE_ENGINE = mybir.EngineType.PE
ACT_ENGINE = mybir.EngineType.Activation

P = 128
TILES = 4
GE = TILES * P
SG = 4
SE = SG * GE
W = 64
EPS = 1e-5
NEWTON = 3
NEWTON_START = 0x5f375a86
RSTD_STEPS = 3 + 3 * NEWTON
NT = 125
BT = 4
XCH = 10
PARTS = 3
ORDER = [0, 2, 1, 3]


def gnn_kernel(nc, x, src, dst, edge_attr, edge_weight, We1, be1, We2, be2, Wt, bt, Wn1, bn1, Wn2, bn2, out):
    N, C = x.shape
    E, F = edge_attr.shape
    SUPERS = 1 + E // SE
    G = SUPERS * SG
    SHARED = SUPERS * SE - E
    BODY = 2 * SG
    TURNS = SUPERS // 2
    SPAN_TABLES = 3
    SUFFIX_STEPS = next(n for n in range(16) if 1 << n >= SUPERS)
    RAW = BODY - 3
    EARLY = 2
    SPLIT_STEPS = 2 * PARTS
    ROWS = [P, G - P]
    NTILES = N // NT
    BLOCKS = [(t, min(BT, NTILES - t)) for t in range(0, NTILES, BT)]
    CHUNKS = NTILES // XCH
    BN = BT * NT
    FULL = NTILES // BT
    DOUBLINGS = next(n for n in range(16) if P << n >= N + W)
    ZERO = -(-(N + W) // len(BLOCKS))
    assert C == P and F == 64 and E % SE and SUPERS % 2 == 0 and P < G <= 2 * P
    assert N % NT == 0 and NTILES % XCH == 0 and 0 < SHARED <= GE
    assert FULL < len(BLOCKS) and TILES * C == BT * C

    table = nc.dram_tensor("node_table", (N, C), F32).ap()
    t_parts = nc.dram_tensor("t_parts", (PARTS, G, GE), BF16).ap()
    spans_dram = nc.dram_tensor("spans_dram", (G, 2), I32).ap()

    with ExitStack() as ctx:
        def sb(name, shape, dt=F32):
            return ctx.enter_context(nc.sbuf_tensor(name, shape, dt))

        def psum(name, shape):
            return ctx.enter_context(nc.psum_tensor(name, shape, F32))

        def sem(name):
            return ctx.enter_context(nc.semaphore(name))

        ident = sb("ident", [P, P])
        ones_parts = sb("ones_parts", [PARTS, P], BF16)
        node_ids = sb("node_ids", [P, N + W])
        we1 = sb("we1", [P, C])
        we2 = sb("we2", [P, C])
        wn1 = sb("wn1", [P, 2, C])
        wn2 = sb("wn2", [P, C])
        be1_c, be2_c, wt_c, bt_c = (sb(n, [P, 1]) for n in ("be1_c", "be2_c", "wt_c", "bt_c"))
        bn1_all = sb("bn1_all", [P, C])
        bn2_all = sb("bn2_all", [P, C])
        x_sb = sb("x_sb", [NT, NTILES, C])
        table_own = sb("table_own", [P, 3, BT * C])
        sums = sb("sums", [P, N + W])
        counts = sb("counts", [P, N + W])
        zero_c = sb("zero_c", [P, 1])
        src_rows = sb("src_rows", [P, 2, GE], I32)
        dst_rows = sb("dst_rows", [P, 2, GE], I32)
        t_split = sb("t_split", [P, 2, PARTS, GE], BF16)
        span_f = sb("span_f", [P, 2, 2])
        span_i = sb("span_i", [P, 2, 2], I32)
        src_e = sb("src_e", [P, G + BODY, TILES])
        dst_e = sb("dst_e", [P, G, TILES])
        spans = sb("spans", [1, G, 2], I32)
        widths = sb("widths", [1, G])
        widest = sb("widest", [1, SUPERS], I32)
        least_from = sb("least_from", [1, 2, 2 * SUPERS])
        lowest = sb("lowest", [1, SUPERS], I32)
        ea = [sb(f"ea{i}", [P, SG, TILES * F]) for i in range(2)]
        tp = [sb(f"tp{i}", [PARTS, SG, GE], BF16) for i in range(2)]
        idx = sb("idx", [P, BODY, TILES], I32)
        eaT = sb("eaT", [P, 2, 2, P])
        h1 = sb("h1", [P, 2, 2, GE // 2])
        tw = sb("tw", [P, 2, GE])
        efw = sb("efw", [P, 2, GE])
        gathered = sb("gathered", [P, BODY, GE])
        xgT = sb("xgT", [P, GE])
        pre = sb("pre", [P, 2, GE])
        h = sb("h", [P, BODY, GE])
        onehot = sb("onehot", [P, 2, TILES, W])
        onehot_more = sb("onehot_more", [P, TILES, W])
        hits = sb("hits", [P, 2, W])
        hits_more = sb("hits_more", [P, W])
        ids_f = h[:, 0:4, :].rearrange("p (a b) e -> p a b e", a=2)
        t_left = h[:, 4:6, :]
        t_rows = h[:, 6:8, :]
        table_sb = ([gathered[0:NT, place, :] for place in range(RAW, BODY)] + [pre[0:NT, b, :] for b in range(2)]
                    + [table_own[0:NT, b, :] for b in range(3)])
        TB = len(table_sb)
        staged_sums, staged_counts = table_own[:, 0, 0:BN], table_own[:, 1, 0:BN]
        y_rows = table_own[0:NT, 2, :].rearrange("p (t c) -> p t c", c=C)
        xT = efw[:, :, :].rearrange("p b (t n) -> p b t n", t=BT)

        psT = psum("psT", [P, 2, P])
        psH = psum("psH", [P, 2, 512])
        psB = psum("psB", [P, GE])
        psE = psum("psE", [P, GE])
        psM = psum("psM", [P, GE])
        psA = psum("psA", [P, 512])
        psX = psum("psX", [P, 512])
        xT_banks, table_banks = [psX, psE], [psM, psA]

        wn1_in, weights_in, dst_in, t_in = (sem(n) for n in ("wn1_in", "weights_in", "dst_in", "t_in"))
        src_in = [sem(f"src_in{b}") for b in range(2)]
        x_in = [sem(f"x_in{i}") for i in range(CHUNKS)]
        table_out = [sem(f"table_out{i}") for i in range(TB)]
        t_out, span_out, spans_in = sem("t_out"), sem("span_out"), sem("spans_in")
        ea_in = [sem(f"ea_in{i}") for i in range(2)]
        tp_in = [sem(f"tp_in{i}") for i in range(2)]
        gather_in = [sem(f"gather_in{i}") for i in range(BODY)]
        y_out = sem("y_out")
        ident_ready, ones_ready, node_ids_ready, tables_zero = (
            sem(n) for n in ("ident_ready", "ones_ready", "node_ids_ready", "tables_zero"))
        xg_ps, xgT_ready = sem("xg_ps"), sem("xgT_ready")
        xT_ps, xT_ready, table_ps, table_ready = (sem(n) for n in ("xT_ps", "xT_ready", "table_ps", "table_ready"))
        src_cast, dst_cast, dst_masked = sem("src_cast"), sem("dst_cast"), sem("dst_masked")
        ids_ps, src_e_ready, dst_e_ready = sem("ids_ps"), sem("src_e_ready"), sem("dst_e_ready")
        split_step, span_found, span_ready, spans_ready = (
            sem(n) for n in ("split_step", "span_found", "span_ready", "spans_ready"))
        idx_ready = sem("idx_ready")
        eaT_ps, eaT_ready, h1_ps, h1_ready = (sem(n) for n in ("eaT_ps", "eaT_ready", "h1_ps", "h1_ready"))
        t_ps, tw_ready, ef_ps, efw_ready = (sem(n) for n in ("t_ps", "tw_ready", "ef_ps", "efw_ready"))
        msg_ps, pre_ready, h_ready = (sem(n) for n in ("msg_ps", "pre_ready", "h_ready"))
        onehot_ready, hits_ready, counts_added = (sem(n) for n in ("onehot_ready", "hits_ready", "counts_added"))
        sum_ps, sums_added = sem("sum_ps"), sem("sums_added")
        more_onehot, more_hits, more_counted, more_sum, more_added = (
            sem(n) for n in ("more_onehot", "more_hits", "more_counted", "more_sum", "more_added"))
        staged, lowest_step = sem("staged"), sem("lowest_step")

        class Room:

            def __init__(self, name, n, free, bank, sums, counts, y, x_at):
                self.bank, self.sums, self.counts, self.y, self.x_at = bank, sums, counts, y, x_at
                self.stats, self.mean_var = sb(f"{name}_stats", [NT, n, 6]), sb(f"{name}_mean_var", [NT, n, 2])
                self.var, self.half, self.rstd, self.shift = (
                    sb(f"{name}_{what}", [NT, n]) for what in ("var", "half", "rstd", "shift"))
                self.bits = sb(f"{name}_bits", [NT, n], I32)
                self.y_ps, self.y_ready, self.stats_ready, self.moments_ready = (
                    sem(f"{name}_{what}") for what in ("y_ps", "y_ready", "stats_ready", "moments_ready"))
                self.rstd_step, self.shift_ready, self.y_done = (
                    sem(f"{name}_{what}") for what in ("rstd_step", "shift_ready", "y_done"))
                self.free = free

        LAST = NTILES - FULL * BT
        full = Room("full", BT, free=1, bank=psX, sums=staged_sums, counts=staged_counts, y=y_rows,
                    x_at=lambda b, t, n: x_sb[:, bass.ds(b * BT + t, n), :])
        last = Room("last", LAST, free=0, bank=psE, sums=sums[:, FULL * BN:N], counts=counts[:, FULL * BN:N],
                    y=x_sb[:, FULL * BT:NTILES, :],
                    x_at=lambda b, t, n: x_sb[:, FULL * BT + t:FULL * BT + t + n, :])

        block = ctx.enter_context(nc.Block())

        x_tiles = x.rearrange("(t n) c -> n t c", n=NT)
        out_tiles = out.rearrange("(t n) c -> n t c", n=NT)
        table_tiles = table.rearrange("(t n) c -> n t c", n=NT)

        def wait(eng, semaphore, value):
            if not (isinstance(value, int) and value <= 0):
                eng.wait_ge(semaphore, value)

        def wait_table(eng):
            for r in range(TB):
                eng.wait_ge(table_out[r], 16 * len(BLOCKS[r::TB]))

        def live(i, k, lag):
            return not isinstance(i, int) or (k >= lag if i == 0 else k < lag)

        def raw(i, g):
            return isinstance(i, int) and i == 0 and 0 <= g < RAW

        def main_loop(eng, step, depth, finish, finish_last):
            for k in range(EARLY, BODY):
                step(0, k)
            with eng.Fori(1, TURNS) as i:
                for k in range(BODY):
                    step(i, k)
                    finish(i, k)
            for k in range(BODY):
                if k < depth:
                    step(TURNS, k)
                finish(TURNS, k)
                if k >= depth - 1:
                    finish_last(k - (depth - 1))

        LOOP_STEPS = dict(stage=0, product=1, y=2, start=4, scale=5, rows=6, other_rows=7)
        END_STEPS = dict(stage=0, product=1, y=1, start=2, scale=3, rows=3, other_rows=3)

        def is_step(i, k, part):
            return k == (END_STEPS if isinstance(i, int) and i == TURNS else LOOP_STEPS)[part]

        def count_blocks(eng, name):
            blocks = eng.alloc_register(name)
            eng.reg_mov(blocks, 0)
            return blocks

        def lowest_of(engine, i):
            return nc.values_load(lowest[0:1, bass.ds(i * 2 - 1, 1)], engines=(engine,), min_val=0, max_val=N - 1)

        def finish_one(eng, blocks, low, work, last):
            b = eng.snap(blocks, min_val=0, max_val=FULL)
            with eng.If(low - b * BN >= BN):
                work(eng.snap(blocks, min_val=0, max_val=FULL - 1))
                if last:
                    eng.reg_add(blocks, blocks, 1)

        def finish_rest(eng, blocks, work):
            b = eng.snap(blocks, min_val=0, max_val=FULL)
            with eng.If(b < FULL):
                with eng.Fori(b, FULL) as b:
                    work(b)

        def widest_of(engine, m):
            return nc.values_load(widest[0:1, bass.ds(m, 1)], engines=(engine,), min_val=0, max_val=N - 1)

        def span_of(engine, g):
            return (nc.values_load(spans[0:1, bass.ds(g, 1), 0], engines=(engine,), min_val=0, max_val=N - 1),
                    nc.values_load(spans[0:1, bass.ds(g, 1), 1], engines=(engine,), min_val=0, max_val=N - 1))

        def least_of(engine, g):
            return nc.values_load(spans[0:1, bass.ds(g, 1), 0], engines=(engine,), min_val=0, max_val=N - 1)

        def by_group(a):
            return [a[E - SE:E].rearrange("(g e) -> g e", e=GE),
                    a[0:(P - SG) * GE].rearrange("(g e) -> g e", e=GE),
                    a[(P - SG) * GE:(G - SG) * GE].rearrange("(g e) -> g e", e=GE)]

        col, row = "(c a) -> c a", "(a c) -> a c"
        loads_first = [(wn1[:, :, :], Wn1.rearrange("(a k) c -> k a c", k=P)),
                       (bn1_all[:, :], bn1.rearrange(row, a=1).to_broadcast([P, C]))]
        loads_act = [(we1[0:F, :], We1), (we1[F:2 * F, :], We1), (be1_c[:, :], be1.rearrange(col, a=1)),
                     (we2[:, :], We2)]
        loads_sp = [(bt_c[:, :], bt.rearrange(col, a=1)), (wt_c[:, :], Wt.rearrange("a c -> c a")),
                    (be2_c[:, :], be2.rearrange(col, a=1)), (wn2[:, :], Wn2),
                    (bn2_all[:, :], bn2.rearrange(row, a=1).to_broadcast([P, C]))]
        N_WEIGHTS = len(loads_act) + len(loads_sp)

        @block.sync
        def _(sp):
            def load_x(c):
                sp.dma_start(x_sb[:, c * XCH:(c + 1) * XCH, :],
                             x_tiles[:, c * XCH:(c + 1) * XCH, :]).then_inc(x_in[c], 16)

            def load_rows(tile, a, landed, parts=(0, 1, 2)):
                last, first, second = by_group(a)
                places = [(tile[0:SG, 0, :], last), (tile[SG:P, 0, :], first), (tile[0:ROWS[1], 1, :], second)]
                for n in parts:
                    sp.dma_start(*places[n]).then_inc(landed, 16)

            load_rows(src_rows, src, src_in[0], (0, 1))
            load_x(0)
            load_rows(src_rows, src, src_in[1], (2,))
            load_rows(dst_rows, dst, dst_in)
            load_x(1)
            load_rows(t_rows, edge_weight, t_in)
            for c in range(2, CHUNKS):
                load_x(c)
            for to, of in loads_sp:
                sp.dma_start(to, of).then_inc(weights_in, 16)

            def load_edges(slot, start):
                sp.dma_start(ea[slot][:, :, :],
                             edge_attr[bass.ds(start, SE), :].rearrange("(g p j) f -> p g (j f)", p=P, j=TILES))\
                    .then_inc(ea_in[slot], 16)

            def load_t(m, slot):
                sp.dma_start(tp[slot][:, :, :], t_parts[:, bass.ds(m * SG, SG), :]).then_inc(tp_in[slot], 16)

            load_edges(0, E - SE)

            def store_parts(r):
                sp.wait_ge(split_step, SPLIT_STEPS * (r + 1))
                sp.dma_start(t_parts[:, r * P:r * P + ROWS[r], :].rearrange("k g e -> g k e"),
                             t_split[0:ROWS[r], r, :, :]).then_inc(t_out, 16)

            for b, (t0, n) in enumerate(BLOCKS):
                sp.wait_ge(table_ready, b + 1)
                sp.dma_start(table_tiles[:, t0:t0 + n, :],
                             table_sb[b % TB][:, 0:n * C].rearrange("p (t c) -> p t c", c=C))\
                    .then_inc(table_out[b % TB], 16)
                if b == 2:
                    sp.wait_ge(span_ready, 2)
                    for r in range(2):
                        sp.dma_start(spans_dram[r * P:r * P + ROWS[r], :], span_i[0:ROWS[r], r, :])\
                            .then_inc(span_out, 16)
                if b == 5:
                    sp.wait_ge(span_out, 32)
                    sp.dma_start(spans[:, :, :], spans_dram.rearrange("(a g) k -> a g k", a=1)).then_inc(spans_in, 16)
                if b == 6:
                    store_parts(0)
                if b == 9:
                    sp.wait_ge(t_out, 16)
                    load_t(0, 0)

            load_edges(1, 0)
            load_t(1, 1)
            store_parts(1)
            sp.wait_ge(t_out, 32)

            def load_super(m, slot, start):
                sp.wait_ge(eaT_ps, (m - 1) * SG)
                sp.wait_ge(t_ps, (m - 1) * SG)
                load_edges(slot, start)
                load_t(m, slot)

            with sp.Fori(1, TURNS) as i:
                load_super(i * 2, 0, i * (2 * SE) - SE)
                load_super(i * 2 + 1, 1, i * (2 * SE))

        @block.gpsimd
        def _(pool):
            pool.memset(ident[:, :], 0.0).then_inc(ident_ready, 1)
            pool.wait_ge(ident_ready, 1)
            pool.affine_select(out=ident[:, :], in_=ident[:, :], compare_op=ALU.not_equal, fill=1.0,
                               base=0, pattern=[[-1, P]], channel_multiplier=1).then_inc(ident_ready, 1)
            pool.iota(node_ids[:, 0:P], pattern=[[1, P]], base=0, channel_multiplier=0,
                      allow_small_or_imprecise_dtypes=True).then_inc(node_ids_ready, 1)
            pool.memset(ones_parts[:, :], 1.0).then_inc(ones_ready, 1)
            pool.memset(zero_c[:, :], 0.0).then_inc(ones_ready, 1)
            pool.memset(sums[:, :], 0.0).then_inc(tables_zero, 1)

            def gather_group(place, rows):
                for t in range(TILES):
                    pool.indirect_dma_start(
                        gathered[:, place, t * C:(t + 1) * C], None, rows,
                        bass.IndirectOffsetOnAxis(idx[:, place, t:t + 1], 0)).then_inc(gather_in[place], 16)

            pool.wait_ge(idx_ready, BODY)
            for place in range(BODY):
                if place == RAW:
                    wait_table(pool)
                gather_group(place, x if place < RAW else table)

            with pool.Fori(1, TURNS) as i:
                for place in range(BODY):
                    g = i * BODY + place
                    pool.wait_ge(pre_ready, g - (BODY - 1))
                    pool.nop(nofuse=True)
                    pool.wait_ge(idx_ready, g + 1)
                    pool.nop(nofuse=True)
                    gather_group(place, table)

        @block.scalar
        def _(act):
            for to, of in loads_first:
                act.dma_start(to, of).then_inc(wn1_in, 16)
            for to, of in loads_act:
                act.dma_start(to, of).then_inc(weights_in, 16)

            act.wait_ge(ones_ready, 2)
            nc.scalar.activation(full.shift[:, 0:1], zero_c[0:NT, :], ACT.Sigmoid).then_inc(full.y_done, 1)

            def zero_counts(b):
                at = slice(b * ZERO, min(N + W, (b + 1) * ZERO))
                nc.scalar.activation(counts[:, at], zero_c[:, :].to_broadcast([P, at.stop - at.start]), ACT.Copy)\
                    .then_inc(tables_zero, 1)

            def step(i, k):
                if live(i, k, 0) and not (isinstance(i, int) and i == TURNS):
                    g = i * BODY + k
                    act.wait_ge(eaT_ps, g + 1)
                    wait(act, h1_ps, g - 1)
                    nc.scalar.activation(eaT[:, k % 2, :, :], psT[:, :, :], ACT.Copy).then_inc(eaT_ready, 1)
                if live(i, k, 1):
                    g = i * BODY + (k - 1)
                    act.wait_ge(h1_ps, g + 1)
                    wait(act, ef_ps, g - 1)
                    nc.scalar.activation(h1[:, (k - 1) % 2, :, :], psH[:, :, 0:GE // 2], ACT.Relu,
                                         bias=be1_c[:, :]).then_inc(h1_ready, 1)
                    act.wait_ge(t_ps, g + 1)
                    wait(act, efw_ready, g - 1)
                    nc.scalar.activation(tw[:, (k - 1) % 2, :], psB[:, :], ACT.Sigmoid, bias=bt_c[:, :],
                                         scale=wt_c[:, :]).then_inc(tw_ready, 1)
                if raw(i, k - 2):
                    act.wait_ge(xg_ps, k - 1)
                    wait(act, msg_ps, k - 2)
                    nc.scalar.activation(xgT[:, :], psX[:, :], ACT.Copy).then_inc(xgT_ready, 1)
                if live(i, k, 3):
                    g = i * BODY + (k - 3)
                    act.wait_ge(pre_ready, g + 1)
                    if (k - 3) % SG == 0:
                        wait(act, sum_ps, g - SG)
                    nc.scalar.activation(h[:, (k - 3) % BODY, :], pre[:, (k - 3) % 2, :], ACT.Relu).then_inc(h_ready, 1)

            for b, (t0, n) in enumerate(BLOCKS):
                act.wait_ge(xT_ps, b + 1)
                if b >= 2:
                    act.wait_ge(table_ps, b - 1)
                nc.scalar.activation(xT[:, b % 2, 0:n, 0:NT],
                                     xT_banks[b % 2][:, :].rearrange("p (t n) -> p t n", t=BT)[:, 0:n, 0:NT],
                                     ACT.Copy).then_inc(xT_ready, 1)
                zero_counts(b)

            act.wait_ge(weights_in, 16 * N_WEIGHTS)
            for k in range(EARLY):
                step(0, k)

            act.wait_ge(split_step, 2 * SPLIT_STEPS)
            act.wait_ge(ids_ps, 4)
            blocks = count_blocks(act, "act_blocks")

            def make_rows(room, b, tiles):
                act.wait_ge(room.shift_ready, b + 1)
                act.nop(nofuse=True)
                for t in tiles:
                    nc.scalar.activation(room.x_at(b, t, 1).rearrange("p a c -> p (a c)"), room.y[:, t, :],
                                         ACT.Identity, bias=room.shift[:, t:t + 1], scale=room.rstd[:, t:t + 1])\
                        .then_inc(room.y_done, 1)

            def store_rows(room, b, first, n):
                act.wait_ge(room.y_done, b * n + (n + room.free))
                act.dma_start(out_tiles[:, bass.ds(first, n), :], room.x_at(b, 0, n)).then_inc(y_out, 16)

            def first_rows(b):
                make_rows(full, b, range(0, BT // 2))

            def other_rows(b):
                make_rows(full, b, range(BT // 2, BT))
                store_rows(full, b, b * BT, BT)

            def finish(i, k):
                if is_step(i, k, "rows"):
                    low["now"] = lowest_of(ACT_ENGINE, i)
                    finish_one(act, blocks, low["now"], first_rows, False)
                if is_step(i, k, "other_rows"):
                    finish_one(act, blocks, low["now"], other_rows, True)

            def finish_last(n):
                if n == 1:
                    make_rows(last, 0, range(LAST))
                    store_rows(last, 0, FULL * BT, LAST)

            def finish_all(b):
                first_rows(b)
                other_rows(b)

            low = {}
            act.wait_ge(spans_ready, SPAN_TABLES)
            main_loop(act, step, 3, finish, finish_last)
            finish_rest(act, blocks, finish_all)
            act.wait_ge(y_out, 16 * (FULL + 1))

        @block.tensor
        def _(pe):
            def transpose_ids(a, b):
                rows = ids_f[0:ROWS[b], a, b, :].rearrange("g (p j) -> g j p", j=TILES)
                for q, j in enumerate(ORDER):
                    mm = nc.tensor.transpose(psH[:, b, q * P:q * P + ROWS[b]], rows[:, j, :],
                                             ident[0:ROWS[b], 0:ROWS[b]])
                mm.then_inc(ids_ps, 1)

            pe.wait_ge(ident_ready, 2)
            pe.wait_ge(src_cast, 1)
            transpose_ids(0, 0)

            def transpose_x(b):
                t0, n = BLOCKS[b]
                for c in range(t0 // XCH, (t0 + n - 1) // XCH + 1):
                    pe.wait_ge(x_in[c], 16)
                if b >= 2:
                    pe.wait_ge(xT_ready, b - 1)
                for q in range(n):
                    mm = nc.tensor.transpose(xT_banks[b % 2][:, q * P:q * P + NT], x_sb[:, t0 + q, :],
                                             ident[0:NT, 0:NT])
                mm.then_inc(xT_ps, 1)

            def multiply_x(b):
                t0, n = BLOCKS[b]
                pe.wait_ge(xT_ready, b + 1)
                if b >= 2:
                    pe.wait_ge(table_ready, b - 1)
                for q in range(n):
                    mm = nc.tensor.matmul(table_banks[b % 2][0:NT, q * P:(q + 1) * P], xT[:, b % 2, q, 0:NT],
                                          wn1[:, 0, :], start=True, stop=True)
                mm.then_inc(table_ps, 1)

            windows = pe.alloc_register("pe_windows")
            pe.reg_mov(windows, 0)

            def more_windows(m, g, place, wide):
                with pe.If(wide >= W):
                    wait(pe, sums_added, g)
                    for q in range(SG):
                        lo, hi = span_of(PE_ENGINE, m * SG + q)
                        with pe.If(hi - lo >= W):
                            with pe.Fori(lo + W, hi + 1, W):
                                pe.reg_add(windows, windows, 1)
                                n = pe.snap(windows, min_val=1)
                                pe.wait_ge(more_onehot, n)
                                for t in range(TILES):
                                    mm = nc.tensor.matmul(psA[:, 0:W], h[:, place + q, t * C:(t + 1) * C],
                                                          onehot_more[:, t, :], start=(t == 0), stop=(t == TILES - 1))
                                mm.then_inc(more_sum, 1)
                                pe.wait_ge(more_added, n)

            def step(i, k):
                if isinstance(i, int) and i == 0 and k == BODY - 1:
                    pe.wait_ge(xgT_ready, RAW)
                if live(i, k, 0) and not (isinstance(i, int) and i == TURNS):
                    g = i * BODY + k
                    if k % SG == 0:
                        pe.wait_ge(ea_in[k // SG], i * 16 + 16)
                    wait(pe, eaT_ready, g)
                    for a in range(2):
                        mm = nc.tensor.transpose(psT[:, a, :], ea[k // SG][:, k % SG, a * P:(a + 1) * P], ident[:, :])
                    mm.then_inc(eaT_ps, 1)
                if live(i, k, 1):
                    g = i * BODY + (k - 1)
                    pe.wait_ge(eaT_ready, g + 1)
                    wait(pe, h1_ready, g)
                    for a in range(2):
                        mm = nc.tensor.matmul(psH[:, a, 0:GE // 2], we1[a * F:(a + 1) * F, :],
                                              eaT[a * F:(a + 1) * F, (k - 1) % 2, :, :], start=True, stop=True)
                    mm.then_inc(h1_ps, 1)
                    if (k - 1) % SG == 0:
                        pe.wait_ge(tp_in[(k - 1) // SG % 2], i * 16 + 16)
                    wait(pe, tw_ready, g)
                    nc.tensor.matmul(psB[:, :], ones_parts[:, :], tp[(k - 1) // SG % 2][:, (k - 1) % SG, :],
                                     start=True, stop=True).then_inc(t_ps, 1)
                if live(i, k, 2):
                    g = i * BODY + (k - 2)
                    pe.wait_ge(h1_ready, g + 1)
                    wait(pe, efw_ready, g)
                    nc.tensor.matmul(psE[:, :], we2[:, :], h1[:, (k - 2) % 2, :, :], start=True, stop=True)\
                        .then_inc(ef_ps, 1)
                if raw(i, k - 2):
                    place = k - 2
                    pe.wait_ge(gather_in[place], 16 * TILES)
                    wait(pe, xgT_ready, place)
                    for t in range(TILES):
                        mm = nc.tensor.transpose(psX[:, t * P:(t + 1) * P], gathered[:, place, t * C:(t + 1) * C],
                                                 ident[:, :])
                    mm.then_inc(xg_ps, 1)
                if live(i, k, 3):
                    g = i * BODY + (k - 3)
                    pe.wait_ge(efw_ready, g + 1)
                    wait(pe, pre_ready, g)
                    if raw(i, k - 3):
                        pe.wait_ge(xgT_ready, k - 2)
                    for t in range(TILES):
                        at = slice(t * P, (t + 1) * P)
                        mm = nc.tensor.matmul(psM[:, at], efw[:, (k - 3) % 2, at], wn1[:, 1, :],
                                              start=True, stop=not raw(i, k - 3))
                        if raw(i, k - 3):
                            mm = nc.tensor.matmul(psM[:, at], xgT[:, at], wn1[:, 0, :], start=False, stop=True)
                    mm.then_inc(msg_ps, 1)
                if live(i, k, 4):
                    g = i * BODY + (k - 4)
                    if k % SG == SG - 1:
                        m = i * 2 + (k - 4) // SG
                        if isinstance(m, int) and m == 0:
                            pe.wait_ge(spans_ready, SPAN_TABLES)
                        wide = widest_of(PE_ENGINE, m)
                    pe.wait_ge(h_ready, g + 1)
                    if k % SG == SG - 1:
                        more_windows(m, g, (k - 4) // SG % 2 * SG, wide)
                    pe.wait_ge(onehot_ready, g + 1)
                    wait(pe, sums_added, g)
                    for t in range(TILES):
                        mm = nc.tensor.matmul(psA[:, 0:W], h[:, (k - 4) % BODY, t * C:(t + 1) * C],
                                              onehot[:, (k - 4) % 2, t, :], start=(t == 0), stop=(t == TILES - 1))
                    mm.then_inc(sum_ps, 1)

            pe.wait_ge(src_cast, 2)
            transpose_ids(0, 1)
            transpose_x(0)
            pe.wait_ge(wn1_in, 32)
            for b in range(len(BLOCKS)):
                if b + 1 < len(BLOCKS):
                    transpose_x(b + 1)
                multiply_x(b)
                if b == 3:
                    pe.wait_ge(dst_masked, 1)
                    for r in range(2):
                        pe.wait_ge(src_e_ready, r + 1)
                        transpose_ids(1, r)
                if b == len(BLOCKS) - EARLY:
                    pe.wait_ge(weights_in, 16 * N_WEIGHTS)
                    pe.wait_ge(dst_e_ready, 2)
                    pe.wait_ge(ones_ready, 1)
                if b >= len(BLOCKS) - EARLY:
                    step(0, b - (len(BLOCKS) - EARLY))

            pe.wait_ge(xT_ready, len(BLOCKS))
            pe.wait_ge(table_ready, len(BLOCKS))
            blocks = count_blocks(pe, "pe_blocks")

            def multiply_node_sums(room, n):
                for q in range(n):
                    at = slice(q * NT, (q + 1) * NT)
                    rows = room.bank[0:NT, q * P:(q + 1) * P]
                    nc.tensor.matmul(rows, room.sums[:, at], wn2[:, :], start=True, stop=False)
                    mm = nc.tensor.matmul(rows, room.counts[:, at], bn2_all[:, :], start=False, stop=True)
                mm.then_inc(room.y_ps, 1)

            def multiply_block(b):
                pe.wait_ge(staged, b * 2 + 2)
                multiply_node_sums(full, BT)

            def finish(i, k):
                if is_step(i, k, "product"):
                    finish_one(pe, blocks, lowest_of(PE_ENGINE, i), multiply_block, True)

            def finish_last(n):
                if n == 0:
                    pe.wait_ge(sums_added, G)
                    pe.wait_ge(counts_added, G)
                    multiply_node_sums(last, LAST)

            main_loop(pe, step, 4, finish, finish_last)
            finish_rest(pe, blocks, multiply_block)

        @block.vector
        def _(dve):
            def cast(a, rows, b, done):
                nc.vector.tensor_copy(ids_f[0:ROWS[b], a, b, :], rows[0:ROWS[b], b, :]).then_inc(done, 1)

            def spread(ids, b, ready):
                nc.vector.tensor_copy(ids[:, b * P:b * P + ROWS[b], :].rearrange("p g q -> p q g"),
                                      psH[:, b, :].rearrange("p (q g) -> p q g", q=TILES)[:, :, 0:ROWS[b]])\
                    .then_inc(ready, 1)

            def stage_indices(g, place, n):
                nc.vector.tensor_copy(idx[:, place:place + n, :], src_e[:, bass.ds(g, n), :]).then_inc(idx_ready, n)

            def double_ids(n):
                have = P << n
                more = min(have, N + W - have)
                dve.wait_ge(node_ids_ready, 1 + n)
                nc.vector.tensor_scalar(node_ids[:, have:have + more], node_ids[:, 0:more], float(have), None, ALU.add)\
                    .then_inc(node_ids_ready, 1)

            for n in range(DOUBLINGS - 1):
                double_ids(n)

            nc.vector.memset(src_e[:, G:G + BODY, :], 0.0)
            dve.wait_ge(src_in[0], 32)
            cast(0, src_rows, 0, src_cast)
            dve.wait_ge(ids_ps, 1)
            spread(src_e, 0, src_e_ready)
            dve.wait_ge(src_e_ready, 1)
            stage_indices(0, 0, BODY)
            dve.wait_ge(src_in[1], 16)
            cast(0, src_rows, 1, src_cast)
            dve.wait_ge(ids_ps, 2)
            spread(src_e, 1, src_e_ready)

            dve.wait_ge(dst_in, 48)
            for b in range(2):
                cast(1, dst_rows, b, dst_cast)
            dve.wait_ge(dst_cast, 2)
            double_ids(DOUBLINGS - 1)

            def find_spans(b):
                for n, op in enumerate((ALU.min, ALU.max)):
                    nc.vector.tensor_reduce(span_f[0:ROWS[b], b, n:n + 1], ids_f[0:ROWS[b], 1, b, :], AX_X, op)\
                        .then_inc(span_found, 1)

            def split_t(s):
                b, part = s // SPLIT_STEPS, s % SPLIT_STEPS
                R = ROWS[b]
                left = t_left[0:R, b, :]
                if part > 0:
                    dve.wait_ge(split_step, s)
                if part == 0:
                    ins = nc.vector.tensor_copy(
                        left.rearrange("g (o i p) -> g o i p", o=2, i=2),
                        t_rows[0:R, b, :].rearrange("g (p i o) -> g o i p", i=2, o=2))
                elif part % 2:
                    ins = nc.vector.tensor_copy(t_split[0:R, b, part // 2, :], left)
                else:
                    ins = nc.vector.tensor_tensor(left, left, t_split[0:R, b, part // 2 - 1, :], ALU.subtract)
                ins.then_inc(split_step, 1)

            dve.wait_ge(wn1_in, 32)
            for b, (t0, n) in enumerate(BLOCKS):
                dve.wait_ge(table_ps, b + 1)
                if b >= TB:
                    dve.wait_ge(table_out[b % TB], b // TB * 16)
                nc.vector.tensor_tensor(table_sb[b % TB][:, 0:n * C].rearrange("p (t c) -> p t c", c=C),
                                        table_banks[b % 2][0:NT, 0:n * C].rearrange("p (t c) -> p t c", c=C),
                                        bn1_all[0:NT, :].rearrange("p (a c) -> p a c", a=1).to_broadcast([NT, n, C]),
                                        ALU.add).then_inc(table_ready, 1)
                if b == 0:
                    find_spans(0)
                    dve.wait_ge(span_found, 2)
                    nc.vector.memset(ids_f[0:1, 1, 0, 0:SHARED], -1.0).then_inc(dst_masked, 1)
                if b == 1:
                    find_spans(1)
                if b == 2:
                    dve.wait_ge(span_found, 4)
                    for r in range(2):
                        nc.vector.tensor_copy(span_i[0:ROWS[r], r, :], span_f[0:ROWS[r], r, :]).then_inc(span_ready, 1)
                    dve.wait_ge(t_in, 48)
                    split_t(0)
                if b >= 2:
                    split_t(b - 1)
                if b == 6:
                    for r in range(2):
                        dve.wait_ge(ids_ps, 3 + r)
                        spread(dst_e, r, dst_e_ready)
            dve.wait_ge(spans_in, 16)
            nc.vector.tensor_tensor(widths[:, :], spans[:, :, 1], spans[:, :, 0], ALU.subtract).then_inc(spans_ready, 1)
            dve.wait_ge(spans_ready, 1)
            nc.vector.tensor_reduce(widest[:, :], widths[:, :].rearrange("a (m g) -> a m g", g=SG), AX_X, ALU.max)\
                .then_inc(spans_ready, 1)
            nc.vector.memset(least_from[:, :, :], float(N)).then_inc(lowest_step, 1)
            dve.wait_ge(lowest_step, 1)
            nc.vector.tensor_reduce(least_from[:, 0, 0:SUPERS], spans[:, :, 0].rearrange("a (m g) -> a m g", g=SG),
                                    AX_X, ALU.min).then_inc(lowest_step, 1)
            for n in range(SUFFIX_STEPS):
                dve.wait_ge(lowest_step, n + 2)
                nc.vector.tensor_tensor(least_from[:, (n + 1) % 2, 0:SUPERS], least_from[:, n % 2, 0:SUPERS],
                                        least_from[:, n % 2, 1 << n:(1 << n) + SUPERS], ALU.min)\
                    .then_inc(lowest_step, 1)
            dve.wait_ge(lowest_step, SUFFIX_STEPS + 2)
            nc.vector.tensor_copy(lowest[:, :], least_from[:, SUFFIX_STEPS % 2, 0:SUPERS]).then_inc(spans_ready, 1)
            dve.wait_ge(node_ids_ready, 1 + DOUBLINGS)
            dve.wait_ge(dst_e_ready, 2)
            dve.wait_ge(weights_in, 16 * N_WEIGHTS)
            dve.wait_ge(tables_zero, 1 + len(BLOCKS))
            dve.wait_ge(spans_ready, SPAN_TABLES)

            windows = dve.alloc_register("dve_windows")
            dve.reg_mov(windows, 0)

            def find_hits(to, lo, g):
                return nc.vector.tensor_tensor(
                    to, node_ids[:, bass.ds(lo, W)].rearrange("p (a w) -> p a w", a=1).to_broadcast([P, TILES, W]),
                    dst_e[:, bass.ds(g, 1), :].rearrange("p a t -> p (a t)").rearrange("p (t a) -> p t a", a=1)
                    .to_broadcast([P, TILES, W]), ALU.is_equal)

            def add_tiles(to, hot):
                return nc.vector.tensor_reduce(to, hot.rearrange("p t w -> p w t"), AX_X, ALU.add)

            def add_at(to, lo, what):
                at = to[:, bass.ds(lo, W)]
                return nc.vector.tensor_tensor(at, at, what, ALU.add)

            def more_windows(m, g, counted, wide):
                with dve.If(wide >= W):
                    wait(dve, sums_added, g)
                    wait(dve, counts_added, counted)
                    for q in range(SG):
                        lo, hi = span_of(DVE_ENGINE, m * SG + q)
                        with dve.If(hi - lo >= W):
                            with dve.Fori(lo + W, hi + 1, W) as at:
                                dve.reg_add(windows, windows, 1)
                                n = dve.snap(windows, min_val=1)
                                find_hits(onehot_more[:, :, :], at, m * SG + q).then_inc(more_onehot, 1)
                                dve.wait_ge(more_onehot, n)
                                add_tiles(hits_more[:, :], onehot_more[:, :, :]).then_inc(more_hits, 1)
                                dve.wait_ge(more_hits, n)
                                add_at(counts, at, hits_more[:, :]).then_inc(more_counted, 1)
                                dve.wait_ge(more_sum, n)
                                add_at(sums, at, psA[:, 0:W]).then_inc(more_added, 1)
                                dve.wait_ge(more_counted, n)
                                dve.wait_ge(more_added, n)

            least, ahead = {}, {}

            def step(i, k):
                if live(i, k, 3):
                    g = i * BODY + (k - 3)
                    if not (k - 3) % BODY in ahead:
                        ahead[(k - 3) % BODY] = least_of(DVE_ENGINE, g)
                    least[(k - 3) % BODY] = lo = ahead.pop((k - 3) % BODY)
                    wait(dve, sum_ps, g - 1)
                    find_hits(onehot[:, (k - 3) % 2, :, :], lo, g).then_inc(onehot_ready, 1)
                if live(i, k, 2):
                    g = i * BODY + (k - 2)
                    dve.wait_ge(ef_ps, g + 1)
                    dve.wait_ge(tw_ready, g + 1)
                    wait(dve, msg_ps, g - 1)
                    nc.vector.scalar_tensor_tensor(efw[:, (k - 2) % 2, :], psE[:, :], be2_c[:, :],
                                                   tw[:, (k - 2) % 2, :], ALU.add, ALU.mult).then_inc(efw_ready, 1)
                if live(i, k, 4) and k % SG == SG - 1:
                    m = i * 2 + (k - 4) // SG
                    wide = widest_of(DVE_ENGINE, m)
                if live(i, k, 3):
                    g = i * BODY + (k - 3)
                    dve.wait_ge(onehot_ready, g + 1)
                    add_tiles(hits[:, (k - 3) % 2, :], onehot[:, (k - 3) % 2, :, :]).then_inc(hits_ready, 1)
                    dve.wait_ge(msg_ps, g + 1)
                    place = (k - 3) % BODY
                    dve.wait_ge(gather_in[place], (i if k < 3 else i + 1) * (16 * TILES))
                    wait(dve, h_ready, g - 1)
                    if isinstance(i, int) and i == 0 and k == 3:
                        wait_table(dve)
                    tiled = "p (t c) -> p t c"
                    if raw(i, k - 3):
                        rest = bn1_all[:, :].rearrange("p (a c) -> p a c", a=1).to_broadcast([P, TILES, C])
                    else:
                        rest = gathered[:, place, :].rearrange(tiled, c=C)
                    nc.vector.tensor_tensor(pre[:, (k - 3) % 2, :].rearrange(tiled, c=C),
                                            psM[:, :].rearrange(tiled, c=C), rest, ALU.add).then_inc(pre_ready, 1)
                    if k < BODY - 1 and live(i, k + 1, 3):
                        ahead[(k - 2) % BODY] = least_of(DVE_ENGINE, g + 1)
                    if not (isinstance(i, int) and i == TURNS):
                        stage_indices(g + BODY, place, 1)
                    dve.wait_ge(hits_ready, g + 1)
                    wait(dve, counts_added, g)
                    add_at(counts, lo, hits[:, (k - 3) % 2, :]).then_inc(counts_added, 1)
                if live(i, k, 4):
                    g = i * BODY + (k - 4)
                    if k % SG == SG - 1:
                        behind = isinstance(i, int) and i == TURNS
                        more_windows(m, g, G if behind else g + 2, wide)
                    lo = least_of(DVE_ENGINE, g) if k == 0 or (k - 4) % BODY not in least else least[(k - 4) % BODY]
                    dve.wait_ge(sum_ps, g + 1)
                    wait(dve, sums_added, g)
                    add_at(sums, lo, psA[:, 0:W]).then_inc(sums_added, 1)

            blocks = count_blocks(dve, "dve_blocks")

            def stage(b):
                nc.vector.tensor_copy(staged_sums, sums[:, bass.ds(b * BN, BN)]).then_inc(staged, 1)
                nc.vector.tensor_copy(staged_counts, counts[:, bass.ds(b * BN, BN)]).then_inc(staged, 1)


            def make_y(room, b, n):
                dve.wait_ge(room.y_ps, b + 1)
                nc.vector.scalar_tensor_tensor(room.y, room.x_at(b, 0, n), 2.0,
                                               room.bank[0:NT, 0:n * C].rearrange("p (t c) -> p t c", c=C),
                                               ALU.mult, ALU.add).then_inc(room.y_ready, 1)
                dve.wait_ge(room.y_ready, b + 1)
                dve.nop(nofuse=True)
                for t in range(n):
                    nc.vector.bn_stats(room.stats[:, t, :], room.y[:, t, :]).then_inc(room.stats_ready, 1)

            def start_scale(room, b, n):
                dve.wait_ge(room.stats_ready, b * n + n)
                dve.nop(nofuse=True)
                for t in range(n):
                    nc.vector.bn_aggr(room.mean_var[:, t, :], room.stats[:, t, :]).then_inc(room.moments_ready, 1)
                dve.wait_ge(room.moments_ready, b * n + n)
                nc.vector.tensor_scalar(room.var[:, :], room.mean_var[:, :, 1], EPS, None, ALU.add)\
                    .then_inc(room.rstd_step, 1)
                dve.wait_ge(room.rstd_step, b * RSTD_STEPS + 1)
                nc.vector.tensor_scalar(room.bits[:, :], room.var[:, :].bitcast(I32), 1, None, ALU.logical_shift_right)\
                    .then_inc(room.rstd_step, 1)
                dve.wait_ge(room.rstd_step, b * RSTD_STEPS + 2)
                nc.vector.tensor_scalar(room.rstd[:, :].bitcast(I32), room.bits[:, :], -1.0, float(NEWTON_START),
                                        ALU.mult, ALU.add).then_inc(room.rstd_step, 1)

            def newton(room, b, n):
                before = b * RSTD_STEPS + (3 + 3 * n)
                dve.wait_ge(room.rstd_step, before)
                nc.vector.tensor_tensor(room.half[:, :], room.rstd[:, :], room.var[:, :], ALU.mult)\
                    .then_inc(room.rstd_step, 1)
                dve.wait_ge(room.rstd_step, before + 1)
                nc.vector.scalar_tensor_tensor(room.half[:, :], room.half[:, :], -0.5, room.rstd[:, :],
                                               ALU.mult, ALU.mult)\
                    .then_inc(room.rstd_step, 1)
                dve.wait_ge(room.rstd_step, before + 2)
                nc.vector.scalar_tensor_tensor(room.rstd[:, :], room.half[:, :], 1.5, room.rstd[:, :],
                                               ALU.add, ALU.mult)\
                    .then_inc(room.rstd_step, 1)

            def find_shift(room, b):
                dve.wait_ge(room.rstd_step, b * RSTD_STEPS + RSTD_STEPS)
                nc.vector.scalar_tensor_tensor(room.shift[:, :], room.mean_var[:, :, 0], -1.0, room.rstd[:, :],
                                               ALU.mult, ALU.mult).then_inc(room.shift_ready, 1)

            def block_y(b):
                dve.wait_ge(full.y_done, b * BT + full.free)
                dve.nop(nofuse=True)
                make_y(full, b, BT)

            def block_start(b):
                start_scale(full, b, BT)
                newton(full, b, 0)

            def block_scale(b):
                for n in range(1, NEWTON):
                    newton(full, b, n)
                find_shift(full, b)

            low = {}

            def finish(i, k):
                if is_step(i, k, "stage"):
                    dve.wait_ge(sums_added, i * BODY + (k - 3))
                    dve.wait_ge(counts_added, i * BODY + (k - 2))
                    low["now"] = lowest_of(DVE_ENGINE, i)
                    finish_one(dve, blocks, low["now"], stage, False)
                if is_step(i, k, "y"):
                    finish_one(dve, blocks, low["now"], block_y, False)
                if is_step(i, k, "start"):
                    finish_one(dve, blocks, low["now"], block_start, False)
                if is_step(i, k, "scale"):
                    finish_one(dve, blocks, low["now"], block_scale, True)

            def finish_last(n):
                if n == 1:
                    make_y(last, 0, LAST)
                if n == 2:
                    start_scale(last, 0, LAST)
                    for m in range(NEWTON):
                        newton(last, 0, m)
                    find_shift(last, 0)

            def finish_all(b):
                stage(b)
                block_y(b)
                block_start(b)
                block_scale(b)

            main_loop(dve, step, 4, finish, finish_last)
            finish_rest(dve, blocks, finish_all)


_INS = ['x', 'src', 'dst', 'edge_attr_64', 'edge_weight', 'L0_gnn_We1', 'L0_gnn_be1', 'L0_gnn_We2', 'L0_gnn_be2',
        'L0_gnn_Wt', 'L0_gnn_bt', 'L0_gnn_Wn1', 'L0_gnn_bn1', 'L0_gnn_Wn2', 'L0_gnn_bn2']
_OUT = ((6250, 128), 'float32')


def kernel(**inputs):
    import numpy as _np
    import concourse.bacc as _bacc
    from concourse import mybir as _mybir
    from concourse.bass_utils import run_bass_kernel_spmd as _run

    nc = _bacc.Bacc("TRN2", target_bir_lowering=False, num_devices=1)
    arrays, args = {}, []
    for name in _INS:
        a = _np.ascontiguousarray(inputs[name])
        arrays[f"in_{name}"] = a
        args.append(nc.dram_tensor(f"in_{name}", a.shape, _mybir.dt.from_np(a.dtype), kind="ExternalInput").ap())
    shape, dtype = _OUT
    args.append(nc.dram_tensor("out_y", shape, _mybir.dt.from_np(_np.dtype(dtype)), kind="ExternalOutput").ap())
    gnn_kernel(nc, *args)
    r = _run(nc, [arrays], core_ids=[0])
    return r.results[0]["out_y"]
```
